# Optimizing a Trainium2 kernel written in Bass

```python
import numpy as np
import jax
import jax.numpy as jnp

def _softmax(x, axis=-1):
    return jax.nn.softmax(x, axis=axis)

def _gelu(x):
    return jax.nn.gelu(x, approximate=True)

def _silu(x):
    return jax.nn.silu(x)

def _sigmoid(x):
    return jax.nn.sigmoid(x)

def _layernorm(x, axis=-1, eps=1e-05):
    m = jnp.mean(x, axis=axis, keepdims=True)
    v = jnp.var(x, axis=axis, keepdims=True)
    return (x - m) / jnp.sqrt(v + eps)

def _scatter_add(tgt, idx, src, axis=0):
    return tgt.at[idx].add(src)

def _segment_sum(src, seg, n):
    return jax.ops.segment_sum(src, seg, n)
kernel_name = 'mk_sandwich_d1_jaxref_r8_2ba04a'

def setup_inputs(seed: int=0):
    np.random.seed(seed)
    _w = jnp.asarray

    def _L0_attn_setup():
        import jax, jax.numpy as jnp
        import numpy as np
        DIM = 512
        N_HEADS = 32
        N_KV_HEADS = 8
        HEAD_DIM = DIM // N_HEADS
        N_REP = N_HEADS // N_KV_HEADS
        THETA = 10000.0
        B, S = (4, 128)

        def _rope_cos_sin(seq_len):
            freqs = 1.0 / THETA ** (jnp.arange(0, HEAD_DIM, 2, dtype=jnp.float32) / HEAD_DIM)
            t = jnp.arange(seq_len, dtype=jnp.float32)
            ang = jnp.outer(t, freqs)
            return (jnp.cos(ang), jnp.sin(ang))

        def _apply_rope(x, cos, sin):
            xr = x[..., 0::2]
            xi = x[..., 1::2]
            c = cos[None, :, None, :]
            s = sin[None, :, None, :]
            out_r = xr * c - xi * s
            out_i = xr * s + xi * c
            return jnp.stack([out_r, out_i], axis=-1).reshape(x.shape)
        key = jax.random.key(seed)
        ks = jax.random.split(key, 5)
        sc = 1.0 / np.sqrt(DIM).astype(np.float32)
        x = jax.random.normal(ks[0], (B, S, DIM), jnp.float32)
        wq = jax.random.normal(ks[1], (DIM, N_HEADS * HEAD_DIM), jnp.float32) * sc
        wk = jax.random.normal(ks[2], (DIM, N_KV_HEADS * HEAD_DIM), jnp.float32) * sc
        wv = jax.random.normal(ks[3], (DIM, N_KV_HEADS * HEAD_DIM), jnp.float32) * sc
        wo = jax.random.normal(ks[4], (N_HEADS * HEAD_DIM, DIM), jnp.float32) * sc
        return {'x': x, 'wq': wq, 'wk': wk, 'wv': wv, 'wo': wo}
    _L0_attn_in = _L0_attn_setup()

    def _L0_ffn_setup():
        import jax, jax.numpy as jnp
        import numpy as np
        BATCH, TOK, DIM, OUT = (4, 256, 512, 512)
        E, R, TOP_K = (8, 16, 2)
        SCALING = 16.0 / R
        key = jax.random.key(seed)
        ks = jax.random.split(key, 6)
        return {'x': jax.random.normal(ks[0], (BATCH, TOK, DIM), dtype=jnp.float32), 'W_base': jax.random.normal(ks[1], (OUT, DIM), dtype=jnp.float32) / np.sqrt(DIM), 'b_base': jax.random.normal(ks[2], (OUT,), dtype=jnp.float32) * 0.01, 'W_gate': jax.random.normal(ks[3], (E, DIM), dtype=jnp.float32) * 0.01, 'A': jax.random.normal(ks[4], (E, R, DIM), dtype=jnp.float32) / np.sqrt(DIM), 'B': jax.random.normal(ks[5], (OUT, OUT // OUT * R * 0 + R), dtype=jnp.float32)[None].repeat(E, 0) * 0.0 + jax.random.normal(ks[5], (E, OUT, R), dtype=jnp.float32) * 0.02}
    _L0_ffn_in = _L0_ffn_setup()
    _d = {'L0_attn_x': _L0_attn_in['x'], 'L0_attn_wq': _L0_attn_in['wq'], 'L0_attn_wk': _L0_attn_in['wk'], 'L0_attn_wv': _L0_attn_in['wv'], 'L0_attn_wo': _L0_attn_in['wo'], 'L0_ffn_W_base': _L0_ffn_in['W_base'], 'L0_ffn_b_base': _L0_ffn_in['b_base'], 'L0_ffn_W_gate': _L0_ffn_in['W_gate'], 'L0_ffn_A': _L0_ffn_in['A'], 'L0_ffn_B': _L0_ffn_in['B']}
    _x0 = _d['L0_attn_x']
    _d['L0_attn_x'] = jax.random.normal(jax.random.fold_in(jax.random.key(seed), 1), (4, 256, 512), dtype=_x0.dtype)
    del _x0
    return _d

def reference(L0_attn_x, L0_attn_wq, L0_attn_wk, L0_attn_wv, L0_attn_wo, L0_ffn_W_base, L0_ffn_b_base, L0_ffn_W_gate, L0_ffn_A, L0_ffn_B):

    def _L0_attn_ref(x, wq, wk, wv, wo):
        import jax, jax.numpy as jnp
        import numpy as np
        DIM = 512
        N_HEADS = 32
        N_KV_HEADS = 8
        HEAD_DIM = DIM // N_HEADS
        N_REP = N_HEADS // N_KV_HEADS
        THETA = 10000.0
        B, S = (4, 128)

        def _rope_cos_sin(seq_len):
            freqs = 1.0 / THETA ** (jnp.arange(0, HEAD_DIM, 2, dtype=jnp.float32) / HEAD_DIM)
            t = jnp.arange(seq_len, dtype=jnp.float32)
            ang = jnp.outer(t, freqs)
            return (jnp.cos(ang), jnp.sin(ang))

        def _apply_rope(x, cos, sin):
            xr = x[..., 0::2]
            xi = x[..., 1::2]
            c = cos[None, :, None, :]
            s = sin[None, :, None, :]
            out_r = xr * c - xi * s
            out_i = xr * s + xi * c
            return jnp.stack([out_r, out_i], axis=-1).reshape(x.shape)
        bsz, seq_len, _ = x.shape
        q = (x @ wq).reshape(bsz, seq_len, N_HEADS, HEAD_DIM)
        k = (x @ wk).reshape(bsz, seq_len, N_KV_HEADS, HEAD_DIM)
        v = (x @ wv).reshape(bsz, seq_len, N_KV_HEADS, HEAD_DIM)
        cos, sin = _rope_cos_sin(seq_len)
        q = _apply_rope(q, cos, sin)
        k = _apply_rope(k, cos, sin)
        k = jnp.repeat(k, N_REP, axis=2)
        v = jnp.repeat(v, N_REP, axis=2)
        scores = jnp.einsum('bqhd,bkhd->bhqk', q, k) / np.float32(np.sqrt(HEAD_DIM))
        mask = jnp.triu(jnp.full((seq_len, seq_len), -jnp.inf, dtype=scores.dtype), k=1)
        scores = scores + mask
        attn = jax.nn.softmax(scores.astype(jnp.float32), axis=-1).astype(q.dtype)
        out = jnp.einsum('bhqk,bkhd->bqhd', attn, v).reshape(bsz, seq_len, N_HEADS * HEAD_DIM)
        return out @ wo

    def _L0_ffn_ref(x, W_base, b_base, W_gate, A, B):
        import jax, jax.numpy as jnp
        import numpy as np
        BATCH, TOK, DIM, OUT = (4, 256, 512, 512)
        E, R, TOP_K = (8, 16, 2)
        SCALING = 16.0 / R
        result = jnp.einsum('bnd,od->bno', x, W_base) + b_base
        logits = jnp.einsum('bnd,ed->bne', x, W_gate)
        probs = jax.nn.softmax(logits.astype(jnp.float32), axis=-1)
        top_p, top_i = jax.lax.top_k(probs, TOP_K)
        top_p = top_p / jnp.sum(top_p, axis=-1, keepdims=True)
        top_p = top_p.astype(x.dtype)
        route_w = jnp.sum(jax.nn.one_hot(top_i, E, dtype=x.dtype) * top_p[..., None], axis=-2)
        h = jnp.einsum('bnd,erd->bner', x, A)
        hw = h * route_w[..., None]
        delta = jnp.einsum('bner,eor->bno', hw, B)
        return result + delta * SCALING
    x = L0_attn_x
    x = x + _layernorm(_L0_attn_ref(_layernorm(x, axis=-1), L0_attn_wq, L0_attn_wk, L0_attn_wv, L0_attn_wo), axis=-1)
    x = x + _layernorm(_L0_ffn_ref(_layernorm(x, axis=-1), L0_ffn_W_base, L0_ffn_b_base, L0_ffn_W_gate, L0_ffn_A, L0_ffn_B), axis=-1)
    return x

_drawn_inputs = setup_inputs


def setup_inputs(seed=0):
    import zlib

    import numpy as np

    out = dict(_drawn_inputs(seed))
    spreads = {}
    factors = {'L0_ffn_b_base': 8.0}
    for name, (base, spread) in spreads.items():
        noise = np.random.default_rng([zlib.crc32(name.encode()), seed]).standard_normal(out[name].shape)
        drawn = base * np.exp(spread * noise) if base else spread * noise
        out[name] = jnp.asarray(drawn.astype(out[name].dtype))
    for name, factor in factors.items():
        out[name] = (out[name] * factor).astype(out[name].dtype)
    return out
```

```python
from contextlib import ExitStack

import numpy as np

import concourse.bass as bass
from concourse import mybir

F32 = mybir.dt.float32
BF16 = mybir.dt.bfloat16
U32 = mybir.dt.uint32
ALU = mybir.AluOpType
ACT = mybir.ActivationFunctionType
AX = mybir.AxisListType

P = 128
BATCH, SEQ, DIM = 4, 256, 512
HEADS, KV_HEADS, HEAD_DIM = 32, 8, 16
REP = HEADS // KV_HEADS
FREQS = HEAD_DIM // 2
EXPERTS, RANK = 8, 16
EPS = 1e-5
TOKENS = BATCH * SEQ
TILES = TOKENS // P
KC = DIM // P
HALF = TOKENS // 2
GROUP_KV = 4
GROUP_HEADS = GROUP_KV * REP
GROUPS = BATCH * KV_HEADS // GROUP_KV
UNITS = BATCH * KV_HEADS
PARTS = 3
Q_PART = (0, 0, 0, 1, 1, 2)
K_PART = (0, 1, 2, 0, 1, 0)
TERMS = len(Q_PART)
SROWS = TERMS * HEAD_DIM
TROWS = SROWS + PARTS
RING = 4
PRING = 8
ST_LAG = 7
MAX_LAG = 5
PV_LAG = 12
STEPS = 4 * (GROUPS - 1) + PV_LAG + 1
CAT = DIM + EXPERTS * RANK + EXPERTS
CATH = CAT // 2
YB = DIM - CATH
MASKED = -(2.0 ** 127)


def build(nc, x, wq, wk, wv, wo, wcat, lora_b, bias, tables, ident, maskq, iota, out):
    ctx = ExitStack()
    with ctx:
        def sb(name, shape, dt=F32):
            return ctx.enter_context(nc.sbuf_tensor(name, shape, dt))

        def sem(name):
            return ctx.enter_context(nc.semaphore(name))

        x_sb = sb("x_sb", [P, TILES, DIM])
        wq_sb = sb("wq_sb", [P, KC, DIM])
        wk_sb = sb("wk_sb", [P, KC, P])
        wv_sb = sb("wv_sb", [P, KC, P])
        wo_sb = sb("wo_sb", [P, REP, DIM])
        wcat_sb = sb("wcat_sb", [P, KC, CAT])
        lora_b_sb = sb("lora_b_sb", [P, DIM])
        bias_sb = sb("bias_sb", [P, DIM])
        tab_sb = sb("tab_sb", [P, 4, SEQ])
        ident_sb = sb("ident_sb", [P, P])
        ident_bf = sb("ident_bf", [P, P], BF16)
        mask_f = sb("mask_f", [P, P])
        mask_bf = sb("mask_bf", [P, REP, P], BF16)
        iota_sb = sb("iota_sb", [P, EXPERTS])
        eps_sb = sb("eps_sb", [P, 1])
        parts = sb("parts", [P, 2, 2, PARTS, HALF], BF16)
        kst = sb("kst", [P, RING, GROUP_KV, SEQ], BF16)
        v_aug = sb("v_aug", [P, TILES, KV_HEADS, 32])
        o_sb = [sb(f"o_sb{i}", [P, 2, REP, SEQ]) for i in range(2)]
        attn_t = sb("attn_t", [P, REP, TOKENS])
        rden_bc = sb("rden_bc", [P, REP * SEQ])
        den_pk = sb("den_pk", [P, 64])
        rden_pk = sb("rden_pk", [P, 64])
        nmax = sb("nmax", [P, 2, 2, GROUP_HEADS])
        nmax_r = sb("nmax_r", [P, 2, 2, GROUP_HEADS])
        nmax_p = sb("nmax_p", [P, 2, PARTS, GROUP_HEADS], BF16)
        mrow = sb("mrow", [P, 2, SEQ], BF16)
        stats = sb("stats", [P, 4, TILES, 6])
        mv = sb("mv", [P, 4, TILES, 2])
        std = sb("std", [P, 4, TILES])
        rstd = sb("rstd", [P, 4, TILES])
        nmr = sb("nmr", [P, 4, TILES])
        gate = sb("gate", [P, 2, 64])
        gate_i = sb("gate_i", [P, 2, 8], U32)
        region_a = sb("region_a", [P, 12 * 1024])
        xn_t = region_a[:, 0:4096].rearrange("p (c n) -> p c n", c=KC)
        rope_t = region_a[:, 4096:8192].rearrange("p (a b n) -> p a b n", a=2, b=4)
        rot = region_a[:, 8192:10240].rearrange("p (a b n) -> p a b n", a=2, b=2)
        resid = region_a[:, 10240:12288].rearrange("p (a b n) -> p a b n", a=2, b=2)
        probs = region_a[:, :].rearrange("p (u a n) -> p u a n", u=PRING, a=3)
        region_b = sb("region_b", [P, 8192])
        qst = region_b[:, :].bitcast(BF16).rearrange("p (s h n) -> p s h n", s=RING, h=GROUP_HEADS)
        xn_sb = region_b[:, 4096:8192].rearrange("p (t n) -> p t n", t=TILES)
        z1 = region_b[:, 0:1024].rearrange("p (a n) -> p a n", a=2)
        hw = region_b[:, 2048:2304].rearrange("p (a n) -> p a n", a=2)
        hw_t = region_b[:, 2304:2560].rearrange("p (a n) -> p a n", a=2)
        y_sb = region_b[:, 2560:3584].rearrange("p (a n) -> p a n", a=2)
        z2 = region_b[:, 3584:4608].rearrange("p (a n) -> p a n", a=2)
        out_sb = region_b[:, 4608:5632].rearrange("p (a n) -> p a n", a=2)
        xn1_sb = region_b[:, 5632:6656].rearrange("p (a n) -> p a n", a=2)
        xn1_t = region_b[:, 6656:7680].rearrange("p (a c n) -> p a c n", a=2, c=KC)

        ps = ctx.enter_context(nc.psum_tensor("ps", [P, 8, 512], F32))

        q_scr = nc.dram_tensor("q_scr", [2, 2, P, PARTS, TOKENS], BF16, kind="Internal").ap()
        k_scr = nc.dram_tensor("k_scr", [2, 2, P // 2, PARTS, HALF], BF16, kind="Internal").ap()
        r_scr = nc.dram_tensor("r_scr", [BATCH, 4, 2, REP * SEQ], F32, kind="Internal").ap()

        x_loaded = [sem(f"x_loaded{t}") for t in range(TILES)]
        ident_loaded = sem("ident_loaded")
        mask_loaded = sem("mask_loaded")
        wq_loaded = sem("wq_loaded")
        tab_loaded = sem("tab_loaded")
        wkv_loaded = sem("wkv_loaded")
        late_loaded = sem("late_loaded")
        dve_chain = sem("dve_chain")
        pool_const = sem("pool_const")
        bf_const = sem("bf_const")
        var_ready = [sem(f"var_ready{i}") for i in range(4)]
        std_ready = [sem(f"std_ready{i}") for i in range(4)]
        scaled = [sem(f"scaled{i}") for i in range(4)]
        xn_ready = sem("xn_ready")
        xnt_psum = sem("xnt_psum")
        xnt_ready = sem("xnt_ready")
        proj_psum = sem("proj_psum")
        v_psum = sem("v_psum")
        v_ready = sem("v_ready")
        rope_mul = sem("rope_mul")
        rot_r = sem("rot_r")
        rot_i = sem("rot_i")
        part_h = sem("part_h")
        resid1 = [sem("resid1_r"), sem("resid1_i")]
        part_m = sem("part_m")
        part_l = [sem("part_l_r"), sem("part_l_i")]
        scr_written = [sem(f"scr_written{i}") for i in range(5)]
        qk_loaded = [sem(f"qk_loaded{i}") for i in range(RING)]
        s0_psum = sem("s0_psum")
        s12_psum = sem("s12_psum")
        s0_free = sem("s0_free")
        s12_free = sem("s12_free")
        nmax_split = sem("nmax_split")
        mt_psum = sem("mt_psum")
        mrow_ready = sem("mrow_ready")
        mrow_stacked = [sem(f"mrow_stacked{i}") for i in range(2)]
        t_psum = sem("t_psum")
        exp_done = sem("exp_done")
        probs_masked = sem("probs_masked")
        o_psum = sem("o_psum")
        o_ready = sem("o_ready")
        o_sent = [sem(f"o_sent{i}") for i in range(2)]
        den_loaded = sem("den_loaded")
        rden_ready = sem("rden_ready")
        rden_stored = sem("rden_stored")
        rden_loaded = sem("rden_loaded")
        attn_ready = sem("attn_ready")
        wo_psum = sem("wo_psum")
        z1_ready = sem("z1_ready")
        x1_ready = sem("x1_ready")
        xn1_ready = sem("xn1_ready")
        xn1t_psum = sem("xn1t_psum")
        xn1t_ready = sem("xn1t_ready")
        cat_psum = sem("cat_psum")
        gap_ready = sem("gap_ready")
        gexp_ready = sem("gexp_ready")
        hw_ready = sem("hw_ready")
        hwt_psum = sem("hwt_psum")
        hwt_ready = sem("hwt_ready")
        y_psum = sem("y_psum")
        y_ready = sem("y_ready")
        z2_ready = sem("z2_ready")
        out_ready = sem("out_ready")
        out_stored = [sem(f"out_stored{i}") for i in range(2)]

        SETS = [(0, 0), (0, 1), "K", (1, 0), (1, 1)]
        SET_BANKS = [(2, 3), (4, 5), (6, 7), (2, 3), (4, 5)]
        set_of = {s: i for i, s in enumerate(SETS)}
        L_PER_SET = 1

        block = ctx.enter_context(nc.Block())

        @block.sync
        def _(sp):
            sp.dma_start(ident_sb[:, :], ident).then_inc(ident_loaded, 16)
            for t in range(TILES):
                sp.dma_start(x_sb[:, t, :], x[t * P:(t + 1) * P, :]).then_inc(x_loaded[t], 16)
                if t == 1:
                    sp.dma_start(wq_sb[:, :, :], wq.rearrange("(c p) n -> p c n", p=P)).then_inc(wq_loaded, 16)
                if t == 3:
                    sp.dma_start(tab_sb[:, :, :], tables).then_inc(tab_loaded, 16)
            sp.dma_start(mask_f[:, :], maskq).then_inc(mask_loaded, 16)
            sp.dma_start(wk_sb[:, :, :], wk.rearrange("(c p) n -> p c n", p=P)).then_inc(wkv_loaded, 16)
            sp.dma_start(wv_sb[:, :, :], wv.rearrange("(c p) n -> p c n", p=P)).then_inc(wkv_loaded, 16)
            sp.dma_start(wo_sb[:, :, :], wo.rearrange("(r p) n -> p r n", p=P)).then_inc(late_loaded, 16)
            sp.dma_start(wcat_sb[:, :, :], wcat.rearrange("(c p) n -> p c n", p=P)).then_inc(late_loaded, 16)
            sp.dma_start(lora_b_sb[:, :], lora_b).then_inc(late_loaded, 16)
            sp.dma_start(bias_sb[:, :], bias.partition_broadcast(P)).then_inc(late_loaded, 16)
            sp.dma_start(iota_sb[:, :], iota).then_inc(late_loaded, 16)

            def write_set(i):
                for ri in range(2):
                    sp.wait_ge(part_l[ri], i + 1)
                    sp.wait_ge(part_m, 2 * i + 1 + ri)
                    src = parts[:, i % 2, ri, :, :]
                    if SETS[i] == "K":
                        for half in range(2):
                            sp.dma_start(k_scr[half, ri], src[half * 64:half * 64 + 64]).then_inc(scr_written[i], 16)
                    else:
                        half, g = SETS[i]
                        sp.dma_start(q_scr[g, ri, :, :, half * HALF:(half + 1) * HALF], src)\
                            .then_inc(scr_written[i], 16)

            def load_group(gi):
                b, g = divmod(gi, 2)
                half = b // 2
                sp.wait_ge(scr_written[set_of[half, g]], 32)
                sp.wait_ge(scr_written[set_of["K"]], 64)
                if gi >= RING:
                    sp.wait_ge(t_psum, 4 * (gi - RING) + 4)
                elif gi >= 2:
                    sp.wait_ge(xnt_psum, TILES)
                qs = q_scr[g].rearrange("i (f h) a n -> (i f) h a n", h=GROUP_HEADS)
                ks = k_scr[half].rearrange("i (f h) a n -> (i f) h a n", h=KV_HEADS)
                for s in range(TERMS):
                    rows = slice(s * HEAD_DIM, (s + 1) * HEAD_DIM)
                    sp.dma_start(qst[rows, gi % RING, :, :], qs[:, :, Q_PART[s], b * SEQ:(b + 1) * SEQ])\
                        .then_inc(qk_loaded[gi % RING], 16)
                    sp.dma_start(kst[rows, gi % RING, :, :],
                                 ks[:, g * GROUP_KV:(g + 1) * GROUP_KV, K_PART[s], (b % 2) * SEQ:(b % 2 + 1) * SEQ])\
                        .then_inc(qk_loaded[gi % RING], 16)

            def stack_max(gi):
                sp.wait_ge(mrow_ready, gi + 1)
                for a in range(PARTS):
                    sp.dma_start(qst[SROWS + a:SROWS + a + 1, gi % RING, :, :],
                                 mrow[a * GROUP_HEADS:(a + 1) * GROUP_HEADS, gi % 2, :])\
                        .then_inc(mrow_stacked[gi % 2], 16)

            def send_out(b):
                sp.wait_ge(o_ready, 4 * b + 4)
                for j in range(GROUP_KV):
                    if j == 0 and b >= 1:
                        sp.wait_ge(rden_ready, b)
                    sp.dma_start(den_pk[32 * j:32 * j + 32, :],
                                 o_sb[b % 2][32 * j + HEAD_DIM:32 * j + HEAD_DIM + 1, :, :, :]
                                 .rearrange("p g r (c n) -> p (g r c) n", n=64)).then_inc(den_loaded, 16)
                for j in range(GROUP_KV):
                    for g in range(2):
                        row = (g * GROUP_KV + j) * HEAD_DIM
                        sp.dma_start(attn_t[row:row + HEAD_DIM, :, b * SEQ:(b + 1) * SEQ],
                                     o_sb[b % 2][32 * j:32 * j + HEAD_DIM, g, :, :]).then_inc(o_sent[b % 2], 16)

            def spread_rden(b):
                sp.wait_ge(rden_ready, b + 1)
                sp.dma_start(r_scr[b].rearrange("j g (c n) -> (j g c) n", n=64), rden_pk[:, :]).then_inc(rden_stored, 16)
                sp.wait_ge(rden_stored, 16 * (b + 1))
                if b >= 1:
                    sp.wait_ge(attn_ready, b)
                for j in range(GROUP_KV):
                    for g in range(2):
                        row = (g * GROUP_KV + j) * HEAD_DIM
                        sp.dma_start(rden_bc[row:row + HEAD_DIM, :],
                                     r_scr[b, j, g].partition_broadcast(HEAD_DIM)).then_inc(rden_loaded, 16)

            for i in range(3):
                write_set(i)
            for gi in range(RING):
                load_group(gi)
            for i in range(3, 5):
                write_set(i)
            for n in range(MAX_LAG, STEPS + 8):
                gi, r = divmod(n - MAX_LAG, 4)
                if r == 0 and gi < GROUPS:
                    stack_max(gi)
                gi, r = divmod(n - ST_LAG - 4, 4)
                if r == 0 and 0 <= gi < GROUPS - RING:
                    load_group(gi + RING)
                b, r = divmod(n - PV_LAG - 5, 8)
                if r == 0 and 0 <= b < BATCH:
                    send_out(b)
                if r == 1 and 0 <= b < BATCH:
                    spread_rden(b)
            for t in range(TILES):
                sp.wait_ge(out_ready, t + 1)
                sp.dma_start(out[t * P:(t + 1) * P, :], out_sb[:, t % 2, :]).then_inc(out_stored[t % 2], 16)
            for i in range(2):
                sp.wait_ge(out_stored[i], 16 * TILES // 2)

        @block.gpsimd
        def _(pool):
            pool.memset(eps_sb[:, :], EPS).then_inc(pool_const, 1)
            pool.memset(v_aug[:, :, :, :], 0.0).then_inc(pool_const, 1)
            pool.wait_ge(pool_const, 2)
            pool.memset(v_aug[:, :, :, HEAD_DIM:HEAD_DIM + 1], 1.0).then_inc(pool_const, 1)
            pool.wait_ge(pool_const, 3)
            pool.memset(kst[SROWS:TROWS, :, :, :], 1.0).then_inc(pool_const, 1)
            pool.wait_ge(pool_const, 4)
            for i in range(len(SETS)):
                a = i % 2
                pool.wait_ge(rope_mul, i + 1)
                if i >= 2:
                    pool.wait_ge(part_l[1], i - 1)
                    pool.wait_ge(part_h, 2 * (i - 2) + 2)
                pool.tensor_tensor(rot[:, a, 1, :], rope_t[:, a, 2, :], rope_t[:, a, 3, :], ALU.add).then_inc(rot_i, 1)
                pool.wait_ge(rot_i, i + 1)
                pool.wait_ge(part_h, 2 * i + 2)
                pool.tensor_tensor(resid[:, a, 1, :], rot[:, a, 1, :], parts[:, a, 1, 0, :], ALU.subtract)\
                    .then_inc(resid1[1], 1)
                pool.wait_ge(resid1[1], i + 1)
                pool.wait_ge(part_m, 2 * i + 2)
                pool.tensor_tensor(parts[:, a, 1, 2, :], resid[:, a, 1, :], parts[:, a, 1, 1, :], ALU.subtract)\
                    .then_inc(part_l[1], 1)
            for n in range(STEPS + 5):
                u = n - ST_LAG
                if 0 <= u < UNITS:
                    pool.wait_ge(exp_done, u + 1)
                    blocks = probs[:, u % PRING, 0:3:2, :].rearrange("p a (r q) -> p a r q", r=REP)
                    pool.affine_select(out=blocks, in_=blocks, compare_op=ALU.is_ge, fill=0.0, base=0,
                                       pattern=[[0, 2], [0, REP], [1, P]], channel_multiplier=-1)\
                        .then_inc(probs_masked, 1)
                b, r = divmod(n - PV_LAG - 8, 8)
                if r == 0 and 0 <= b < BATCH:
                    pool.wait_ge(o_sent[b % 2], 128 * (b // 2 + 1))
                    pool.wait_ge(rden_loaded, 128 * (b + 1))
                    view = attn_t[:, :, b * SEQ:(b + 1) * SEQ]
                    pool.tensor_tensor(view, view, rden_bc[:, :].rearrange("p (r n) -> p r n", r=REP), ALU.mult)\
                        .then_inc(attn_ready, 1)
            for s in range(TILES + 2):
                if s < TILES:
                    pool.wait_ge(z1_ready, s + 1)
                    pool.tensor_tensor(x_sb[:, s, :], x_sb[:, s, :], z1[:, s % 2, :], ALU.add).then_inc(x1_ready, 1)
                t = s - 2
                if 0 <= t < TILES:
                    pool.wait_ge(z2_ready, t + 1)
                    if t >= 2:
                        pool.wait_ge(out_stored[t % 2], 16 * (t // 2))
                    pool.tensor_tensor(out_sb[:, t % 2, :], x_sb[:, t, :], z2[:, t % 2, :], ALU.add)\
                        .then_inc(out_ready, 1)

        @block.scalar
        def _(act):
            act.wait_ge(pool_const, 1)

            def sqrt(k, t):
                act.wait_ge(var_ready[k], t + 1)
                nc.scalar.activation(std[:, k, t:t + 1], mv[:, k, t, 1:2], ACT.Sqrt, bias=eps_sb[:, 0:1])\
                    .then_inc(std_ready[k], 1)

            def copy_xnt(t):
                act.wait_ge(xnt_psum, t + 1)
                nc.scalar.copy(xn_t[:, :, t * P:(t + 1) * P], ps[:, t % 2, :].rearrange("p (c n) -> p c n", c=KC))\
                    .then_inc(xnt_ready, 1)

            def split_set(i):
                a = i % 2
                for ri, ready in enumerate((rot_r, rot_i)):
                    act.wait_ge(ready, i + 1)
                    if i >= 2:
                        act.wait_ge(scr_written[i - 2], 64 if SETS[i - 2] == "K" else 32)
                    nc.scalar.copy(parts[:, a, ri, 0, :], rot[:, a, ri, :]).then_inc(part_h, 1)
                for ri in range(2):
                    act.wait_ge(resid1[ri], i + 1)
                    nc.scalar.copy(parts[:, a, ri, 1, :], resid[:, a, ri, :]).then_inc(part_m, 1)

            def copy_v(g):
                act.wait_ge(v_psum, g + 1)
                act.wait_ge(pool_const, 3)
                for i in range(4):
                    last = nc.scalar.copy(v_aug[:, 4 * g + i, :, 0:HEAD_DIM],
                                          ps[:, g, i * P:(i + 1) * P].rearrange("p (h d) -> p h d", d=HEAD_DIM))
                last.then_inc(v_ready, 1)

            sqrt(0, 0)
            for t in range(1, 4):
                sqrt(0, t)
                copy_xnt(t - 1)
            for t in range(4, TILES):
                sqrt(0, t)
            copy_xnt(3)
            split_set(0)
            for t in range(4, TILES):
                copy_xnt(t)
            split_set(1)
            split_set(2)
            copy_v(0)
            copy_v(1)
            split_set(3)
            split_set(4)

            for n in range(STEPS):
                gi, r = divmod(n - MAX_LAG, 4)
                if r == 0 and 0 <= gi < GROUPS:
                    act.wait_ge(mt_psum, gi + 1)
                    if gi >= 2:
                        act.wait_ge(mrow_stacked[gi % 2], 48 * (gi // 2))
                    nc.scalar.copy(mrow[0:PARTS * GROUP_HEADS, gi % 2, :],
                                   ps[0:PARTS * GROUP_HEADS, 0, 0:P].bitcast(BF16)).then_inc(mrow_ready, 1)
                u = n - ST_LAG
                if 0 <= u < UNITS:
                    act.wait_ge(t_psum, u + 1)
                    if u == 0:
                        act.wait_ge(proj_psum, len(SETS))
                        act.wait_ge(v_psum, 2)
                        act.wait_ge(part_l[0], len(SETS))
                        act.wait_ge(part_l[1], len(SETS))
                    if u >= PRING:
                        act.wait_ge(o_psum, 2 * ((u - PRING) // 4 + 1))
                    nc.scalar.activation(probs[:, u % PRING, :, :], ps[:, 3:6, :], ACT.Exp,
                                         scale=float(HEAD_DIM) ** -0.5).then_inc(exp_done, 1)
                gi, r = divmod(n - PV_LAG, 4)
                if r == 0 and 0 <= gi < GROUPS:
                    b, g = divmod(gi, 2)
                    for qt in range(2):
                        act.wait_ge(o_psum, 2 * gi + qt + 1)
                        if b >= 2 and qt == 0:
                            act.wait_ge(o_sent[b % 2], 128 * (b // 2))
                            act.wait_ge(den_loaded, 64 * (b - 1))
                        nc.scalar.copy(o_sb[b % 2][:, g, :, qt * P:(qt + 1) * P],
                                       ps[:, 6 + qt, :].rearrange("p (r n) -> p r n", r=REP)).then_inc(o_ready, 1)

            def normalise(k, t, dst, src, ready):
                nc.scalar.activation(dst, src, ACT.Identity, scale=rstd[:, k, t:t + 1],
                                     bias=nmr[:, k, t:t + 1]).then_inc(ready, 1)

            for s in range(TILES + 2):
                if 0 <= s - 1 < TILES:
                    t = s - 1
                    act.wait_ge(xn1t_psum, t + 1)
                    if t >= 2:
                        act.wait_ge(cat_psum, t - 1)
                    nc.scalar.copy(xn1_t[:, t % 2, :, :], ps[:, 2, :].rearrange("p (c n) -> p c n", c=KC))\
                        .then_inc(xn1t_ready, 1)
                if s < TILES:
                    sqrt(1, s)
                    act.wait_ge(scaled[1], s + 1)
                    if s >= 2:
                        act.wait_ge(x1_ready, s - 1)
                    normalise(1, s, z1[:, s % 2, :], ps[:, s % 2, :], z1_ready)
                if 0 <= s - 1 < TILES:
                    t = s - 1
                    act.wait_ge(gap_ready, t + 1)
                    nc.scalar.activation(gate[:, t % 2, 1:2], gate[:, t % 2, 0:1], ACT.Exp).then_inc(gexp_ready, 1)
                if 0 <= s - 2 < TILES:
                    t = s - 2
                    act.wait_ge(hwt_psum, t + 1)
                    if t >= 2:
                        act.wait_ge(y_psum, t - 1)
                    nc.scalar.copy(hw_t[:, t % 2, :], ps[:, 3, 0:P]).then_inc(hwt_ready, 1)
                if s < TILES:
                    sqrt(2, s)
                if 0 <= s - 2 < TILES:
                    t = s - 2
                    sqrt(3, t)
                    act.wait_ge(scaled[3], t + 1)
                    if t >= 2:
                        act.wait_ge(out_ready, t - 1)
                    normalise(3, t, z2[:, t % 2, :], y_sb[:, t % 2, :], z2_ready)

        @block.vector
        def _(dve):
            chained = [0]

            def link(*instructions):
                for ins in instructions:
                    ins.then_inc(dve_chain, 1)
                chained[0] += len(instructions)
                dve.wait_ge(dve_chain, chained[0])

            def ln_stats(k, t, src):
                link(nc.vector.bn_stats(stats[:, k, t, :], src))
                nc.vector.bn_aggr(mv[:, k, t, :], stats[:, k, t, :]).then_inc(var_ready[k], 1)

            def ln_scale(k, t):
                dve.wait_ge(std_ready[k], t + 1)
                link(nc.vector.reciprocal(rstd[:, k, t:t + 1], std[:, k, t:t + 1]))
                nc.vector.scalar_tensor_tensor(out=nmr[:, k, t:t + 1], in0=mv[:, k, t, 0:1], scalar=-1.0,
                                               in1=rstd[:, k, t:t + 1], op0=ALU.mult, op1=ALU.mult)\
                    .then_inc(scaled[k], 1)

            def ln_apply(k, t, dst, src):
                return nc.vector.tensor_scalar(dst, src, mv[:, k, t, 0:1], rstd[:, k, t:t + 1],
                                               ALU.subtract, ALU.mult)

            def input_norm(t):
                ln_scale(0, t)
                ln_apply(0, t, xn_sb[:, t, :], x_sb[:, t, :]).then_inc(xn_ready, 1)

            for t in range(TILES):
                dve.wait_ge(x_loaded[t], 16)
                ln_stats(0, t, x_sb[:, t, :])
                if t >= 1:
                    input_norm(t - 1)
            input_norm(TILES - 1)

            dve.wait_ge(ident_loaded, 16)
            dve.wait_ge(mask_loaded, 16)
            nc.vector.tensor_copy(ident_bf[:, :], ident_sb[:, :]).then_inc(bf_const, 1)
            nc.vector.tensor_copy(mask_bf[:, :, :], mask_f[:, :].unsqueeze(1).broadcast_to([P, REP, P]))\
                .then_inc(bf_const, 1)
            dve.wait_ge(tab_loaded, 16)
            for i, which in enumerate(SETS):
                a = i % 2
                tab = 2 if which == "K" else 0
                cos, sin = (tab_sb[:, tab + j, :].unsqueeze(1).broadcast_to([P, 2, SEQ]) for j in range(2))
                re, im = (ps[:, bank, :].rearrange("p (b n) -> p b n", b=2) for bank in SET_BANKS[i])
                dve.wait_ge(proj_psum, i + 1)
                if i >= 2:
                    dve.wait_ge(rot_r, i - 1)
                    dve.wait_ge(rot_i, i - 1)
                for j, (val, table) in enumerate(((re, cos), (im, sin), (re, sin), (im, cos))):
                    last = nc.vector.tensor_tensor(rope_t[:, a, j, :].rearrange("p (b n) -> p b n", b=2), val, table,
                                                   ALU.mult)
                last.then_inc(rope_mul, 1)
                dve.wait_ge(rope_mul, i + 1)
                if i >= 2:
                    dve.wait_ge(part_l[0], i - 1)
                nc.vector.tensor_tensor(rot[:, a, 0, :], rope_t[:, a, 0, :], rope_t[:, a, 1, :], ALU.subtract)\
                    .then_inc(rot_r, 1)
                dve.wait_ge(part_h, 2 * i + 1)
                nc.vector.tensor_tensor(resid[:, a, 0, :], rot[:, a, 0, :], parts[:, a, 0, 0, :], ALU.subtract)\
                    .then_inc(resid1[0], 1)
                dve.wait_ge(resid1[0], i + 1)
                dve.wait_ge(part_m, 2 * i + 1)
                nc.vector.tensor_tensor(parts[:, a, 0, 2, :], resid[:, a, 0, :], parts[:, a, 0, 1, :], ALU.subtract)\
                    .then_inc(part_l[0], 1)

            for n in range(STEPS + 4):
                if n < UNITS:
                    gi, k = divmod(n, GROUP_KV)
                    heads = slice(k * REP, (k + 1) * REP)
                    dve.wait_ge(s0_psum, n + 1)
                    nc.vector.tensor_reduce(nmax[:, gi % 2, 0, heads], ps[:, 0, :].rearrange("p (r k) -> p r k", r=REP),
                                            AX.X, ALU.max, negate=True).then_inc(s0_free, 1)
                    dve.wait_ge(s12_psum, n + 1)
                    nc.vector.tensor_reduce(nmax[:, gi % 2, 1, heads],
                                            ps[:, 1:3, :].rearrange("p a (r k) -> p r a k", r=REP),
                                            AX.XY, ALU.max, negate=True).then_inc(s12_free, 1)
                    if k == GROUP_KV - 1:
                        full, left = nmax[:, gi % 2, :, :], nmax_r[:, gi % 2, :, :]
                        high, mid, low = (nmax_p[:, :, j, :] for j in range(PARTS))
                        dve.wait_ge(s12_free, n + 1)
                        if gi >= 1:
                            dve.wait_ge(mt_psum, gi)
                        link(nc.vector.tensor_copy(high, full))
                        link(nc.vector.tensor_tensor(left, full, high, ALU.subtract))
                        link(nc.vector.tensor_copy(mid, left))
                        nc.vector.tensor_tensor(low, left, mid, ALU.subtract).then_inc(nmax_split, 1)
                b, r = divmod(n - PV_LAG - 7, 8)
                if r == 0 and 0 <= b < BATCH:
                    dve.wait_ge(den_loaded, 64 * (b + 1))
                    if b >= 1:
                        dve.wait_ge(rden_stored, 16 * b)
                    nc.vector.reciprocal(rden_pk[:, :], den_pk[:, :]).then_inc(rden_ready, 1)

            dve.wait_ge(late_loaded, 80)
            for s in range(TILES + 2):
                t1, t3 = s - 1, s - 2
                if s < TILES:
                    dve.wait_ge(wo_psum, s + 1)
                    ln_stats(1, s, ps[:, s % 2, :])
                if 0 <= t1 < TILES:
                    ga = gate[:, t1 % 2, :]
                    y_bank = ps[:, 5 + 2 * (t1 % 2), :]
                    logits = y_bank[:, YB + EXPERTS * RANK:YB + EXPERTS * RANK + EXPERTS]
                    dve.wait_ge(cat_psum, t1 + 1)
                    link(nc.vector.tensor_copy(ga[:, 48:56], logits))
                    link(nc.vector.max(ga[:, 8:16], ga[:, 48:56]))
                    link(nc.vector.max_index(gate_i[:, t1 % 2, :], ga[:, 8:16], ga[:, 48:56]))
                    link(nc.vector.tensor_copy(ga[:, 16:18], gate_i[:, t1 % 2, 0:2]))
                    nc.vector.tensor_tensor(ga[:, 0:1], ga[:, 9:10], ga[:, 8:9], ALU.subtract).then_inc(gap_ready, 1)
                if s < TILES:
                    ln_scale(1, s)
                if 0 <= t3 < TILES:
                    xb = 4 + 2 * (t3 % 2)
                    dve.wait_ge(y_psum, t3 + 1)
                    if t3 >= 2:
                        dve.wait_ge(z2_ready, t3 - 1)
                    nc.vector.tensor_tensor(y_sb[:, t3 % 2, 0:CATH], ps[:, xb, 0:CATH], bias_sb[:, 0:CATH], ALU.add)
                    nc.vector.tensor_tensor(y_sb[:, t3 % 2, CATH:DIM], ps[:, xb + 1, 0:YB], bias_sb[:, CATH:DIM],
                                            ALU.add).then_inc(y_ready, 1)
                    dve.wait_ge(y_ready, t3 + 1)
                    ln_stats(3, t3, y_sb[:, t3 % 2, :])
                if s < TILES:
                    dve.wait_ge(x1_ready, s + 1)
                    ln_stats(2, s, x_sb[:, s, :])
                if 0 <= t1 < TILES:
                    dve.wait_ge(gexp_ready, t1 + 1)
                    link(nc.vector.tensor_scalar(ga[:, 2:3], ga[:, 1:2], 1.0, None, ALU.add))
                    link(nc.vector.reciprocal(ga[:, 3:4], ga[:, 2:3]))
                    link(nc.vector.tensor_tensor(ga[:, 4:5], ga[:, 1:2], ga[:, 3:4], ALU.mult),
                         nc.vector.tensor_scalar(ga[:, 24:32], iota_sb[:, :], ga[:, 16:17], ga[:, 3:4],
                                                 ALU.is_equal, ALU.mult))
                    link(nc.vector.tensor_scalar(ga[:, 32:40], iota_sb[:, :], ga[:, 17:18], ga[:, 4:5],
                                                 ALU.is_equal, ALU.mult))
                    link(nc.vector.tensor_tensor(ga[:, 40:48], ga[:, 24:32], ga[:, 32:40], ALU.add))
                    if t1 >= 2:
                        dve.wait_ge(hwt_psum, t1 - 1)
                    nc.vector.tensor_tensor(hw[:, t1 % 2, :].rearrange("p (e r) -> p e r", r=RANK),
                                            y_bank[:, YB:YB + EXPERTS * RANK].rearrange("p (e r) -> p e r", r=RANK),
                                            ga[:, 40:48].unsqueeze(2).broadcast_to([P, EXPERTS, RANK]), ALU.mult)\
                        .then_inc(hw_ready, 1)
                if 0 <= t3 < TILES:
                    ln_scale(3, t3)
                if s < TILES:
                    ln_scale(2, s)
                    if s >= 2:
                        dve.wait_ge(xn1t_psum, s - 1)
                    ln_apply(2, s, xn1_sb[:, s % 2, :], x_sb[:, s, :]).then_inc(xn1_ready, 1)

        @block.tensor
        def _(pe):
            pe.wait_ge(ident_loaded, 16)

            def turn_x(t):
                pe.wait_ge(xn_ready, t + 1)
                if t >= 2:
                    pe.wait_ge(xnt_ready, t - 1)
                for c in range(KC):
                    last = nc.tensor.transpose(ps[:, t % 2, c * P:(c + 1) * P], xn_sb[:, t, c * P:(c + 1) * P],
                                               ident_sb[:, :])
                last.then_inc(xnt_psum, 1)

            def project(i):
                if i >= 3:
                    pe.wait_ge(rope_mul, i - 2)
                if SETS[i] == "K":
                    pe.wait_ge(wkv_loaded, 32)
                    pe.wait_ge(xnt_ready, TILES)
                    for ri in range(2):
                        for c in range(KC):
                            for half in range(2):
                                last = nc.tensor.matmul(ps[64 * half:64 * half + 64, SET_BANKS[i][ri], :],
                                                        wk_sb[:, c, 64 * ri:64 * ri + 64],
                                                        xn_t[:, c, half * HALF:(half + 1) * HALF],
                                                        start=(c == 0), stop=(c == KC - 1))
                else:
                    half, g = SETS[i]
                    pe.wait_ge(wq_loaded, 16)
                    pe.wait_ge(xnt_ready, 4 * half + 4)
                    for ri in range(2):
                        col = (2 * g + ri) * P
                        for c in range(KC):
                            last = nc.tensor.matmul(ps[:, SET_BANKS[i][ri], :], wq_sb[:, c, col:col + P],
                                                    xn_t[:, c, half * HALF:(half + 1) * HALF],
                                                    start=(c == 0), stop=(c == KC - 1))
                last.then_inc(proj_psum, 1)

            def project_v():
                for t in range(TILES):
                    for c in range(KC):
                        last = nc.tensor.matmul(ps[:, t // 4, (t % 4) * P:(t % 4 + 1) * P],
                                                xn_t[:, c, t * P:(t + 1) * P], wv_sb[:, c, :],
                                                start=(c == 0), stop=(c == KC - 1))
                    if t % 4 == 3:
                        last.then_inc(v_psum, 1)

            for t in range(4):
                turn_x(t)
            project(0)
            project(1)
            for t in range(4, TILES):
                turn_x(t)
            project(2)
            project_v()
            project(3)
            project(4)

            def scores(n):
                gi, k = divmod(n, GROUP_KV)
                slot = gi % RING
                if k == 0:
                    pe.wait_ge(qk_loaded[slot], 192 * (gi // RING + 1))
                if n == 0:
                    pe.wait_ge(bf_const, 2)
                    pe.wait_ge(v_ready, 2)
                    pe.wait_ge(rope_mul, 5)
                    pe.wait_ge(pool_const, 4)
                else:
                    pe.wait_ge(s0_free, n)
                gj, r = divmod(n - MAX_LAG, 4)
                if r == 0 and 0 <= gj < GROUPS:
                    pe.wait_ge(mrow_ready, gj + 1)
                nc.tensor.matmul(ps[:, 0, :], ident_bf[:, :], mask_bf[:, :, :].rearrange("p r k -> p (r k)"),
                                 start=True, stop=False, skip_group_check=True)
                for r in range(REP):
                    h = k * REP + r
                    last = nc.tensor.matmul(ps[:, 0, r * P:(r + 1) * P], qst[0:SROWS, slot, h, 0:P],
                                            kst[0:SROWS, slot, k, 0:P], start=False, stop=(r == REP - 1),
                                            skip_group_check=True)
                last.then_inc(s0_psum, 1)
                if n >= 1:
                    pe.wait_ge(s12_free, n)
                nc.tensor.matmul(ps[:, 2, :], ident_bf[:, :], mask_bf[:, :, :].rearrange("p r k -> p (r k)"),
                                 start=True, stop=False, skip_group_check=True)
                for r in range(REP):
                    h = k * REP + r
                    for kt in range(2):
                        last = nc.tensor.matmul(ps[:, 1 + kt, r * P:(r + 1) * P], qst[0:SROWS, slot, h, P:2 * P],
                                                kst[0:SROWS, slot, k, kt * P:(kt + 1) * P], start=(kt == 0),
                                                stop=(r == REP - 1), skip_group_check=True)
                last.then_inc(s12_psum, 1)

            def turn_max(gi, n):
                pe.wait_ge(nmax_split, gi + 1)
                pe.wait_ge(s0_free, min(n, UNITS))
                for qt in range(2):
                    last = nc.tensor.transpose(ps[0:PARTS * GROUP_HEADS, 0, qt * 64:(qt + 1) * 64].bitcast(BF16),
                                               nmax_p[:, qt, :, :].rearrange("p a h -> p (a h)"), ident_bf[:, :])
                last.then_inc(mt_psum, 1)

            def scores_t(u):
                gi, k = divmod(u, GROUP_KV)
                slot = gi % RING
                if k == 0:
                    pe.wait_ge(mrow_stacked[gi % 2], 48 * (gi // 2 + 1))
                if u >= 1:
                    pe.wait_ge(exp_done, u)
                for j, (kt, qt) in enumerate(((0, 0), (0, 1), (1, 1))):
                    last = nc.tensor.matmul(ps[:, 3 + j, :], kst[0:TROWS, slot, k, kt * P:(kt + 1) * P],
                                            qst[0:TROWS, slot, k * REP:(k + 1) * REP, qt * P:(qt + 1) * P],
                                            start=True, stop=True)
                last.then_inc(t_psum, 1)

            def attend(gi):
                b, g = divmod(gi, 2)
                pe.wait_ge(probs_masked, 4 * gi + 4)
                for qt in range(2):
                    if gi >= 1:
                        pe.wait_ge(o_ready, 2 * gi - 1 + qt)
                    for kt in range(qt + 1):
                        for j in range(GROUP_KV):
                            u = gi * GROUP_KV + j
                            last = nc.tensor.matmul(ps[32 * j:32 * j + 32, 6 + qt, :],
                                                    v_aug[:, 2 * b + kt, g * GROUP_KV + j, :],
                                                    probs[:, u % PRING, qt + kt, :],
                                                    start=(kt == 0), stop=(kt == qt))
                    last.then_inc(o_psum, 1)

            for n in range(STEPS):
                gi, r = divmod(n - MAX_LAG, 4)
                if r == 0 and 0 <= gi < GROUPS:
                    turn_max(gi, n)
                if n < UNITS:
                    scores(n)
                if 0 <= n - ST_LAG < UNITS:
                    scores_t(n - ST_LAG)
                gi, r = divmod(n - PV_LAG, 4)
                if r == 0 and 0 <= gi < GROUPS:
                    attend(gi)

            pe.wait_ge(late_loaded, 80)
            pe.wait_ge(s12_free, UNITS)
            pe.wait_ge(mrow_ready, GROUPS)
            pe.wait_ge(exp_done, UNITS)
            for s in range(TILES + 2):
                if s < TILES:
                    pe.wait_ge(attn_ready, s // 2 + 1)
                    if s >= 2:
                        pe.wait_ge(z1_ready, s - 1)
                    for r in range(REP):
                        last = nc.tensor.matmul(ps[:, s % 2, :], attn_t[:, r, s * P:(s + 1) * P], wo_sb[:, r, :],
                                                start=(r == 0), stop=(r == REP - 1))
                    last.then_inc(wo_psum, 1)
                t = s - 1
                if 0 <= t < TILES:
                    pe.wait_ge(xn1_ready, t + 1)
                    if t >= 1:
                        pe.wait_ge(xn1t_ready, t)
                    for c in range(KC):
                        last = nc.tensor.transpose(ps[:, 2, c * P:(c + 1) * P], xn1_sb[:, t % 2, c * P:(c + 1) * P],
                                                   ident_sb[:, :])
                    last.then_inc(xn1t_psum, 1)
                    pe.wait_ge(xn1t_ready, t + 1)
                    if t >= 2:
                        pe.wait_ge(y_ready, t - 1)
                    if t == 1:
                        pe.wait_ge(o_ready, 2 * GROUPS)
                    for hf in range(2):
                        for c in range(KC):
                            last = nc.tensor.matmul(ps[:, 4 + 2 * (t % 2) + hf, 0:CATH], xn1_t[:, t % 2, c, :],
                                                    wcat_sb[:, c, hf * CATH:(hf + 1) * CATH],
                                                    start=(c == 0), stop=(hf == 1 and c == KC - 1),
                                                    skip_group_check=True)
                    last.then_inc(cat_psum, 1)
                t = s - 2
                if 0 <= t < TILES:
                    pe.wait_ge(hw_ready, t + 1)
                    if t >= 1:
                        pe.wait_ge(hwt_ready, t)
                    nc.tensor.transpose(ps[:, 3, 0:P], hw[:, t % 2, :], ident_sb[:, :]).then_inc(hwt_psum, 1)
                    pe.wait_ge(hwt_ready, t + 1)
                    nc.tensor.matmul(ps[:, 4 + 2 * (t % 2), 0:CATH], hw_t[:, t % 2, :], lora_b_sb[:, 0:CATH],
                                     start=False, stop=True, skip_group_check=True)
                    nc.tensor.matmul(ps[:, 5 + 2 * (t % 2), 0:YB], hw_t[:, t % 2, :], lora_b_sb[:, CATH:DIM],
                                     start=False, stop=True, skip_group_check=True).then_inc(y_psum, 1)


def rotary_tables():
    freqs = 1.0 / np.float32(10000.0) ** (np.arange(0, HEAD_DIM, 2, dtype=np.float32) / HEAD_DIM)
    angles = (np.arange(SEQ, dtype=np.float32)[:, None] * freqs.astype(np.float32)[None]).astype(np.float32)
    rows_q = np.arange(P) // GROUP_HEADS
    rows_k = (np.arange(P) % 64) // KV_HEADS
    return np.stack([f(angles).T[rows] for rows in (rows_q, rows_k) for f in (np.cos, np.sin)], axis=1)\
        .astype(np.float32)


def kernel(L0_attn_x, L0_attn_wq, L0_attn_wk, L0_attn_wv, L0_attn_wo, L0_ffn_W_base, L0_ffn_b_base, L0_ffn_W_gate,
           L0_ffn_A, L0_ffn_B):
    from concourse import bacc
    from concourse.bass_utils import run_bass_kernel_spmd

    def arr(a):
        return np.asarray(a)

    wq = arr(L0_attn_wq).reshape(DIM, 2, GROUP_HEADS, FREQS, 2).transpose(0, 1, 4, 3, 2).reshape(DIM, DIM)
    wk = arr(L0_attn_wk).reshape(DIM, KV_HEADS, FREQS, 2).transpose(0, 3, 2, 1).reshape(DIM, P)
    wo = arr(L0_attn_wo).reshape(KV_HEADS, REP, HEAD_DIM, DIM).transpose(1, 0, 2, 3).reshape(DIM, DIM)
    wcat = np.concatenate([arr(L0_ffn_W_base).T, arr(L0_ffn_A).reshape(EXPERTS * RANK, DIM).T,
                           arr(L0_ffn_W_gate).T], axis=1)
    lora_b = arr(L0_ffn_B).transpose(0, 2, 1).reshape(EXPERTS * RANK, DIM)
    later = np.arange(P)[None, :] > np.arange(P)[:, None]
    arrays = {
        "x": arr(L0_attn_x).reshape(TOKENS, DIM), "wq": wq, "wk": wk, "wv": arr(L0_attn_wv), "wo": wo,
        "wcat": wcat, "lora_b": lora_b, "bias": arr(L0_ffn_b_base), "tables": rotary_tables(),
        "ident": np.eye(P, dtype=np.float32), "maskq": np.where(later, np.float32(MASKED), np.float32(0)),
        "iota": np.tile(np.arange(EXPERTS, dtype=np.float32), (P, 1)),
    }
    arrays = {n: np.ascontiguousarray(a) for n, a in arrays.items()}
    nc = bacc.Bacc("TRN2", target_bir_lowering=False, num_devices=1)
    args = [nc.dram_tensor(n, a.shape, mybir.dt.from_np(a.dtype), kind="ExternalInput").ap() for n, a in arrays.items()]
    out = nc.dram_tensor("out", [TOKENS, DIM], F32, kind="ExternalOutput").ap()
    build(nc, *args, out)
    r = run_bass_kernel_spmd(nc, [arrays], core_ids=[0])
    return r.results[0]["out"].reshape(BATCH, SEQ, DIM)
```

```python
from contextlib import ExitStack

import numpy as np

import concourse.bass as bass
from concourse import mybir

F32 = mybir.dt.float32
BF16 = mybir.dt.bfloat16
U32 = mybir.dt.uint32
ALU = mybir.AluOpType
ACT = mybir.ActivationFunctionType
AX = mybir.AxisListType

P = 128
BATCH, SEQ, DIM = 4, 256, 512
HEADS, KV_HEADS, HEAD_DIM = 32, 8, 16
REP = HEADS // KV_HEADS
FREQS = HEAD_DIM // 2
EXPERTS, RANK = 8, 16
EPS = 1e-5
TOKENS = BATCH * SEQ
TILES = TOKENS // P
KC = DIM // P
HALF = TOKENS // 2
GROUP_KV = 4
GROUP_HEADS = GROUP_KV * REP
GROUPS = BATCH * KV_HEADS // GROUP_KV
UNITS = BATCH * KV_HEADS
PARTS = 3
RUNS = ((0, 3), (3, 2), (5, 1))
TERMS = 6
SROWS = TERMS * HEAD_DIM
TROWS = SROWS + PARTS
RING = 4
PRING = 8
ST_LAG = 7
MAX_LAG = 5
PV_LAG = 12
STEPS = 4 * (GROUPS - 1) + PV_LAG + 3
EARLY = {UNITS + ST_LAG - 1: 0}
EARLY_OUT = {UNITS + ST_LAG - 4: 0, UNITS + ST_LAG - 2: 1}
LATE_ROPE = {0: (3, 1), 1: (3, 2), 4: (4, 0), 5: (4, 1), 6: (4, 2)}
CAT = DIM + EXPERTS * RANK + EXPERTS
CATH = CAT // 2
YB = DIM - CATH
MASKED = -(2.0 ** 127)


def build(nc, x, wq, wk, wv, wo, wcat, lora_b, bias, tables, ident, maskq, iota, out):
    ctx = ExitStack()
    with ctx:
        def sb(name, shape, dt=F32):
            return ctx.enter_context(nc.sbuf_tensor(name, shape, dt))

        def sem(name):
            return ctx.enter_context(nc.semaphore(name))

        x_sb = sb("x_sb", [P, TILES, DIM])
        wq_sb = sb("wq_sb", [P, KC, DIM])
        wk_sb = sb("wk_sb", [P, KC, P])
        wv_sb = sb("wv_sb", [P, KC, P])
        wo_sb = sb("wo_sb", [P, REP, DIM])
        wcat_sb = sb("wcat_sb", [P, KC, CAT])
        lora_b_sb = sb("lora_b_sb", [P, DIM])
        bias_sb = sb("bias_sb", [P, DIM])
        tab_sb = sb("tab_sb", [P, 4, SEQ])
        ident_sb = sb("ident_sb", [P, P])
        ident_bf = sb("ident_bf", [P, P], BF16)
        mask_f = sb("mask_f", [P, P])
        mask_bf = sb("mask_bf", [P, REP, P], BF16)
        iota_sb = sb("iota_sb", [P, EXPERTS])
        eps_sb = sb("eps_sb", [P, 1])
        parts = sb("parts", [P, 2, 2, PARTS, HALF], BF16)
        kst = sb("kst", [P, RING, GROUP_KV, SEQ], BF16)
        v_aug = sb("v_aug", [P, TILES, KV_HEADS, 32])
        o_sb = sb("o_sb", [P, 2, REP, SEQ])
        attn_t = sb("attn_t", [P, BATCH, REP * SEQ])
        rden_bc = sb("rden_bc", [P, REP * SEQ])
        den_pk = sb("den_pk", [P, 64])
        rden_pk = sb("rden_pk", [P, 64])
        nmax = sb("nmax", [P, 2, 2, GROUP_HEADS])
        nmax_r = sb("nmax_r", [P, 2, 2, GROUP_HEADS])
        nmax_p = sb("nmax_p", [P, 2, PARTS, GROUP_HEADS], BF16)
        mrow = sb("mrow", [P, 2, SEQ], BF16)
        stats = sb("stats", [P, 4, TILES, 6])
        mv = sb("mv", [P, 4, TILES, 2])
        std = sb("std", [P, 4, TILES])
        rstd = sb("rstd", [P, 4, TILES])
        nmr = sb("nmr", [P, 4, TILES])
        unused = sb("unused", [P, 2, TILES])
        gate = sb("gate", [P, 2, 64])
        gate_i = sb("gate_i", [P, 2, 8], U32)
        region_a = sb("region_a", [P, 12 * 1024])
        xn_t = region_a[:, 0:4096].rearrange("p (c n) -> p c n", c=KC)
        rope_t = region_a[:, 4096:8192].rearrange("p (a b n) -> p a b n", a=2, b=4)
        rot = region_a[:, 8192:10240].rearrange("p (a b n) -> p a b n", a=2, b=2)
        resid = region_a[:, 10240:12288].rearrange("p (a b n) -> p a b n", a=2, b=2)
        probs = region_a[:, :].rearrange("p (u a n) -> p u a n", u=PRING, a=3)
        region_b = sb("region_b", [P, 8192])
        qst = region_b[:, :].bitcast(BF16).rearrange("p (s h n) -> p s h n", s=RING, h=GROUP_HEADS)
        xn_sb = region_b[:, 4096:8192].rearrange("p (t n) -> p t n", t=TILES)
        z1 = region_b[:, 0:1024].rearrange("p (a n) -> p a n", a=2)
        xn1_sb = region_b[:, 1024:2048].rearrange("p (a n) -> p a n", a=2)
        hw = region_b[:, 2048:2304].rearrange("p (a n) -> p a n", a=2)
        hw_t = region_b[:, 2304:2560].rearrange("p (a n) -> p a n", a=2)
        xn1_t = region_b[:, 2560:3584].rearrange("p (a c n) -> p a c n", a=2, c=KC)
        y_sb = region_b[:, 3584:4608].rearrange("p (a n) -> p a n", a=2)
        z2 = region_b[:, 4608:5632].rearrange("p (a n) -> p a n", a=2)
        out_sb = region_b[:, 5632:6656].rearrange("p (a n) -> p a n", a=2)

        ps = ctx.enter_context(nc.psum_tensor("ps", [P, 8, 512], F32))

        q_scr = nc.dram_tensor("q_scr", [2, SROWS, GROUP_HEADS, TOKENS], BF16, kind="Internal").ap()
        k_scr = nc.dram_tensor("k_scr", [2, SROWS, KV_HEADS, HALF], BF16, kind="Internal").ap()
        o_scr = nc.dram_tensor("o_scr", [GROUPS, P, REP * SEQ], F32, kind="Internal").ap()
        r_scr = nc.dram_tensor("r_scr", [GROUPS, 64, 64], F32, kind="Internal").ap()

        x_loaded = [sem(f"x_loaded{t}") for t in range(TILES)]
        ident_loaded = sem("ident_loaded")
        mask_loaded = sem("mask_loaded")
        wq_loaded = [sem(f"wq_loaded{g}") for g in range(2)]
        tab_loaded = sem("tab_loaded")
        wk_loaded = sem("wk_loaded")
        wv_loaded = sem("wv_loaded")
        late_loaded = sem("late_loaded")
        dve_chain = sem("dve_chain")
        pool_const = sem("pool_const")
        bf_const = sem("bf_const")
        var_ready = [sem(f"var_ready{i}") for i in range(4)]
        std_ready = [sem(f"std_ready{i}") for i in range(4)]
        scaled = [sem(f"scaled{i}") for i in range(4)]
        xn_ready = sem("xn_ready")
        xnt_psum = sem("xnt_psum")
        xnt_ready = sem("xnt_ready")
        proj_psum = sem("proj_psum")
        v_psum = sem("v_psum")
        v_ready = sem("v_ready")
        rope_mul = sem("rope_mul")
        rot_r = sem("rot_r")
        rot_i = sem("rot_i")
        part_h = sem("part_h")
        resid1 = [sem("resid1_r"), sem("resid1_i")]
        part_m = sem("part_m")
        part_l = [sem("part_l_r"), sem("part_l_i")]
        scr_written = [sem(f"scr_written{i}") for i in range(5)]
        k_written = [sem(f"k_written{i}") for i in range(2)]
        qk_loaded = [sem(f"qk_loaded{i}") for i in range(RING)]
        s0_psum = sem("s0_psum")
        s12_psum = sem("s12_psum")
        s0_free = sem("s0_free")
        s12_free = sem("s12_free")
        nmax_split = sem("nmax_split")
        mt_psum = sem("mt_psum")
        mrow_ready = sem("mrow_ready")
        mrow_stacked = [sem(f"mrow_stacked{i}") for i in range(2)]
        t_psum = sem("t_psum")
        exp_done = sem("exp_done")
        probs_masked = sem("probs_masked")
        o_psum = sem("o_psum")
        o_ready = sem("o_ready")
        o_stored = [sem(f"o_stored{i}") for i in range(2)]
        den_loaded = [sem(f"den_loaded{i}") for i in range(4)]
        num_loaded = [sem(f"num_loaded{i}") for i in range(4)]
        rden_ready = sem("rden_ready")
        rden_stored = [sem(f"rden_stored{i}") for i in range(2)]
        rden_loaded = [sem(f"rden_loaded{i}") for i in range(4)]
        attn_ready = sem("attn_ready")
        wo_psum = sem("wo_psum")
        z1_ready = sem("z1_ready")
        x1_ready = sem("x1_ready")
        xn1_ready = sem("xn1_ready")
        xn1t_psum = sem("xn1t_psum")
        xn1t_ready = sem("xn1t_ready")
        cat_psum = sem("cat_psum")
        gap_ready = sem("gap_ready")
        gexp_ready = sem("gexp_ready")
        hw_ready = sem("hw_ready")
        hwt_psum = sem("hwt_psum")
        hwt_ready = sem("hwt_ready")
        y_psum = sem("y_psum")
        y_ready = sem("y_ready")
        z2_ready = sem("z2_ready")
        out_ready = sem("out_ready")
        out_stored = [sem(f"out_stored{i}") for i in range(2)]

        SETS = [(0, 0), "K", (0, 1), (1, 0), (1, 1)]
        SET_BANKS = [(2, 3), (4, 5), (6, 7), (2, 3), (4, 5)]
        set_of = {s: i for i, s in enumerate(SETS)}
        WRITES_Q = WRITES_K = 16 * 2 * len(RUNS)

        block = ctx.enter_context(nc.Block())

        @block.sync
        def _(sp):
            sp.dma_start(ident_sb[:, :], ident).then_inc(ident_loaded, 16)
            sp.dma_start(x_sb[:, 0, :], x[0:P, :]).then_inc(x_loaded[0], 16)
            sp.dma_start(wv_sb[:, :, :], wv.rearrange("(c p) n -> p c n", p=P)).then_inc(wv_loaded, 16)
            wq_v = wq.rearrange("(c p) n -> p c n", p=P)
            for t in range(1, TILES):
                if t == 4:
                    sp.dma_start(wq_sb[:, :, 0:256], wq_v[:, :, 0:256]).then_inc(wq_loaded[0], 16)
                sp.dma_start(x_sb[:, t, :], x[t * P:(t + 1) * P, :]).then_inc(x_loaded[t], 16)
            sp.dma_start(tab_sb[:, :, :], tables).then_inc(tab_loaded, 16)
            sp.dma_start(wk_sb[:, :, :], wk.rearrange("(c p) n -> p c n", p=P)).then_inc(wk_loaded, 16)
            sp.dma_start(wq_sb[:, :, 256:512], wq_v[:, :, 256:512]).then_inc(wq_loaded[1], 16)
            sp.dma_start(mask_f[:, :], maskq).then_inc(mask_loaded, 16)
            sp.dma_start(wo_sb[:, :, :], wo.rearrange("(r p) n -> p r n", p=P)).then_inc(late_loaded, 16)
            sp.dma_start(wcat_sb[:, :, :], wcat.rearrange("(c p) n -> p c n", p=P)).then_inc(late_loaded, 16)
            sp.dma_start(lora_b_sb[:, :], lora_b).then_inc(late_loaded, 16)
            sp.dma_start(bias_sb[:, :], bias.partition_broadcast(P)).then_inc(late_loaded, 16)
            sp.dma_start(iota_sb[:, :], iota).then_inc(late_loaded, 16)

            def write_q(i):
                half, g = SETS[i]
                dst = q_scr[g].rearrange("(s i f) h n -> i (f h) s n", s=TERMS, i=2)
                for ri in range(2):
                    sp.wait_ge(part_l[ri], i + 1)
                    sp.wait_ge(part_m, 2 * i + 1 + ri)
                    for first, count in RUNS:
                        sp.dma_start(dst[ri, :, first:first + count, half * HALF:(half + 1) * HALF],
                                     parts[:, i % 2, ri, 0:count, :]).then_inc(scr_written[i], 16)

            def write_k(part, half):
                i = set_of["K"]
                first, count = RUNS[part]
                dst = k_scr[half].rearrange("(s i f) h n -> i (f h) s n", s=TERMS, i=2)
                for ri in range(2):
                    if part == 0:
                        sp.wait_ge(part_h, 2 * i + 1 + ri)
                    elif part == 1:
                        sp.wait_ge(part_m, 2 * i + 1 + ri)
                    else:
                        sp.wait_ge(part_l[ri], i + 1)
                    rows = parts[half * 64:half * 64 + 64, i % 2, ri, part:part + 1, :]
                    sp.dma_start(dst[ri, :, first:first + count, :], rows.broadcast_to([64, count, HALF]))\
                        .then_inc(k_written[half], 16)

            def wait_ring(gi):
                if gi >= RING:
                    sp.wait_ge(t_psum, 4 * (gi - RING) + 4)
                elif gi >= 2:
                    sp.wait_ge(xnt_psum, TILES)

            def load_q(gi):
                b, g = divmod(gi, 2)
                sp.wait_ge(scr_written[set_of[b // 2, g]], WRITES_Q)
                wait_ring(gi)
                sp.dma_start(qst[0:SROWS, gi % RING, :, :], q_scr[g, :, :, b * SEQ:(b + 1) * SEQ])\
                    .then_inc(qk_loaded[gi % RING], 16)

            def load_k(gi):
                b, g = divmod(gi, 2)
                sp.wait_ge(k_written[b // 2], WRITES_K)
                wait_ring(gi)
                sp.dma_start(kst[0:SROWS, gi % RING, :, :],
                             k_scr[b // 2, :, g * GROUP_KV:(g + 1) * GROUP_KV, (b % 2) * SEQ:(b % 2 + 1) * SEQ])\
                    .then_inc(qk_loaded[gi % RING], 16)

            def stack_max(gi):
                sp.wait_ge(mrow_ready, gi + 1)
                sp.dma_start(qst[SROWS:TROWS, gi % RING, :, :], mrow[0:PARTS * GROUP_HEADS, gi % 2, :])\
                    .then_inc(mrow_stacked[gi % 2], 16)

            def send_out(gi):
                sp.wait_ge(o_ready, 2 * gi + 2)
                sp.dma_start(o_scr[gi], o_sb[:, gi % 2, :, :].rearrange("p r n -> p (r n)"))\
                    .then_inc(o_stored[gi % 2], 16)

            def fetch_out(gi):
                b, g = divmod(gi, 2)
                rows = slice(64 * g, 64 * g + 64)
                src = o_scr[gi].rearrange("(j e) n -> j e n", j=GROUP_KV)
                sp.wait_ge(o_stored[gi % 2], 16 * (gi // 2 + 1))
                if gi >= 2:
                    sp.wait_ge(rden_ready, gi - 1)
                sp.dma_start(den_pk[rows, :], src[:, HEAD_DIM, :].rearrange("j (c n) -> j c n", n=64))\
                    .then_inc(den_loaded[gi % 4], 16)
                sp.dma_start(attn_t[rows, b, :], src[:, 0:HEAD_DIM, :]).then_inc(num_loaded[gi % 4], 16)

            def store_rden(gi):
                sp.wait_ge(rden_ready, gi + 1)
                sp.dma_start(r_scr[gi], rden_pk[64 * (gi % 2):64 * (gi % 2) + 64, :]).then_inc(rden_stored[gi % 2], 16)

            def spread_rden(gi):
                b, g = divmod(gi, 2)
                sp.wait_ge(rden_stored[g], 16 * (b + 1))
                if b >= 1:
                    sp.wait_ge(attn_ready, b)
                src = r_scr[gi].rearrange("(j c) n -> j (c n)", j=GROUP_KV)
                sp.dma_start(rden_bc[64 * g:64 * g + 64, :],
                             src.unsqueeze(1).broadcast_to([GROUP_KV, HEAD_DIM, REP * SEQ])).then_inc(rden_loaded[gi % 4], 16)

            write_q(0)
            load_q(0)
            load_q(2)
            for part in range(PARTS):
                for half in range(2):
                    write_k(part, half)
            load_k(0)
            load_k(1)
            write_q(2)
            load_q(1)
            load_k(2)
            load_k(3)
            load_q(3)
            write_q(3)
            for n in range(MAX_LAG, STEPS + 5):
                for lag, count, what in ((MAX_LAG, GROUPS, stack_max), (PV_LAG + 3, GROUPS, send_out),
                                         (PV_LAG + 4, GROUPS, fetch_out), (PV_LAG + 6, GROUPS, store_rden),
                                         (PV_LAG + 7, GROUPS, spread_rden)):
                    gi, r = divmod(n - lag, 4)
                    if r == 0 and 0 <= gi < count:
                        what(gi)
                if n == MAX_LAG:
                    write_q(4)
                gi, r = divmod(n - ST_LAG - 4, 4)
                if r == 0 and 0 <= gi < GROUPS - RING:
                    load_k(gi + RING)
                    load_q(gi + RING)
            for t in range(TILES):
                sp.wait_ge(out_ready, t + 1)
                sp.dma_start(out[t * P:(t + 1) * P, :], out_sb[:, t % 2, :]).then_inc(out_stored[t % 2], 16)
            for i in range(2):
                sp.wait_ge(out_stored[i], 16 * TILES // 2)

        @block.gpsimd
        def _(pool):
            pool.memset(eps_sb[:, :], EPS).then_inc(pool_const, 1)
            pool.memset(v_aug[:, :, :, :], 0.0).then_inc(pool_const, 1)
            pool.wait_ge(pool_const, 2)
            pool.memset(v_aug[:, :, :, HEAD_DIM:HEAD_DIM + 1], 1.0).then_inc(pool_const, 1)
            pool.wait_ge(pool_const, 3)
            pool.memset(kst[SROWS:TROWS, :, :, :], 1.0).then_inc(pool_const, 1)
            pool.wait_ge(pool_const, 4)
            for i in range(len(SETS)):
                a = i % 2
                pool.wait_ge(rope_mul, i + 1)
                if i >= 2:
                    pool.wait_ge(part_l[1], i - 1)
                    pool.wait_ge(part_h, 2 * (i - 2) + 2)
                pool.tensor_tensor(rot[:, a, 1, :], rope_t[:, a, 2, :], rope_t[:, a, 3, :], ALU.add).then_inc(rot_i, 1)
                pool.wait_ge(rot_i, i + 1)
                pool.wait_ge(part_h, 2 * i + 2)
                pool.tensor_tensor(resid[:, a, 1, :], rot[:, a, 1, :], parts[:, a, 1, 0, :], ALU.subtract)\
                    .then_inc(resid1[1], 1)
                pool.wait_ge(resid1[1], i + 1)
                pool.wait_ge(part_m, 2 * i + 2)
                pool.tensor_tensor(parts[:, a, 1, 2, :], resid[:, a, 1, :], parts[:, a, 1, 1, :], ALU.subtract)\
                    .then_inc(part_l[1], 1)
            def divide(b):
                for g in range(2):
                    pool.wait_ge(num_loaded[(2 * b + g) % 4], 16 * (b // 2 + 1))
                    pool.wait_ge(rden_loaded[(2 * b + g) % 4], 16 * (b // 2 + 1))
                pool.tensor_tensor(attn_t[:, b, :], attn_t[:, b, :], rden_bc[:, :], ALU.mult).then_inc(attn_ready, 1)

            def residuals(s):
                if s < TILES:
                    pool.wait_ge(z1_ready, s + 1)
                    pool.tensor_tensor(x_sb[:, s, :], x_sb[:, s, :], z1[:, s % 2, :], ALU.add).then_inc(x1_ready, 1)
                t = s - 2
                if 0 <= t < TILES:
                    pool.wait_ge(z2_ready, t + 1)
                    if t >= 2:
                        pool.wait_ge(out_stored[t % 2], 16 * (t // 2))
                    pool.tensor_tensor(out_sb[:, t % 2, :], x_sb[:, t, :], z2[:, t % 2, :], ALU.add)\
                        .then_inc(out_ready, 1)

            for n in range(STEPS):
                u = n - ST_LAG
                if 0 <= u < UNITS:
                    pool.wait_ge(exp_done, u + 1)
                    blocks = probs[:, u % PRING, 0:3:2, :].rearrange("p a (r q) -> p a r q", r=REP)
                    pool.affine_select(out=blocks, in_=blocks, compare_op=ALU.is_ge, fill=0.0, base=0,
                                       pattern=[[0, 2], [0, REP], [1, P]], channel_multiplier=-1)\
                        .then_inc(probs_masked, 1)
                b, r = divmod(n - PV_LAG - 12, 8)
                if r == 0 and 0 <= b < BATCH - 1:
                    divide(b)
                if n in EARLY:
                    residuals(EARLY[n])
            for s in range(1, TILES + 2):
                residuals(s)
                if s == 3:
                    divide(BATCH - 1)

        @block.scalar
        def _(act):
            act.wait_ge(pool_const, 1)

            def sqrt(k, t):
                act.wait_ge(var_ready[k], t + 1)
                nc.scalar.activation(std[:, k, t:t + 1], mv[:, k, t, 1:2], ACT.Sqrt, bias=eps_sb[:, 0:1])\
                    .then_inc(std_ready[k], 1)

            def copy_xnt(t):
                act.wait_ge(xnt_psum, t + 1)
                nc.scalar.copy(xn_t[:, :, t * P:(t + 1) * P], ps[:, t % 2, :].rearrange("p (c n) -> p c n", c=KC))\
                    .then_inc(xnt_ready, 1)

            def split_high(i):
                a = i % 2
                for ri, ready in enumerate((rot_r, rot_i)):
                    act.wait_ge(ready, i + 1)
                    if i >= 2:
                        if SETS[i - 2] == "K":
                            act.wait_ge(k_written[0], WRITES_K)
                            act.wait_ge(k_written[1], WRITES_K)
                        else:
                            act.wait_ge(scr_written[i - 2], WRITES_Q)
                    nc.scalar.copy(parts[:, a, ri, 0, :], rot[:, a, ri, :]).then_inc(part_h, 1)

            def split_middle(i):
                a = i % 2
                for ri in range(2):
                    act.wait_ge(resid1[ri], i + 1)
                    nc.scalar.copy(parts[:, a, ri, 1, :], resid[:, a, ri, :]).then_inc(part_m, 1)

            def copy_v(g):
                act.wait_ge(v_psum, g + 1)
                act.wait_ge(pool_const, 3)
                for i in range(4):
                    last = nc.scalar.copy(v_aug[:, 4 * g + i, :, 0:HEAD_DIM],
                                          ps[:, 6 + g, i * P:(i + 1) * P].rearrange("p (h d) -> p h d", d=HEAD_DIM))
                last.then_inc(v_ready, 1)

            sqrt(0, 0)
            for t in range(1, 4):
                sqrt(0, t)
                copy_xnt(t - 1)
            for t in range(4, TILES):
                sqrt(0, t)
            copy_xnt(3)
            copy_v(0)
            for t in range(4, TILES):
                copy_xnt(t)
            split_high(0)
            split_middle(0)
            copy_v(1)
            for i in range(1, 4):
                split_high(i)
                split_middle(i)

            def normalise(k, t, dst, src, ready):
                nc.scalar.activation(dst, src, ACT.Identity, scale=rstd[:, k, t:t + 1],
                                     bias=nmr[:, k, t:t + 1]).then_inc(ready, 1)

            def bring_table(k, t):
                nc.scalar.activation(unused[:, k, t:t + 1], eps_sb[:, 0:1], (ACT.Exp, ACT.Sqrt)[k])

            def tile_step(s):
                t1, t2 = s - 1, s - 2
                if 0 <= t2 < TILES:
                    act.wait_ge(hwt_psum, t2 + 1)
                    if t2 >= 2:
                        act.wait_ge(y_psum, t2 - 1)
                    nc.scalar.copy(hw_t[:, t2 % 2, :], ps[:, 3, 0:P]).then_inc(hwt_ready, 1)
                if 0 <= t1 < TILES:
                    act.wait_ge(xn1t_psum, t1 + 1)
                    if t1 >= 2:
                        act.wait_ge(cat_psum, t1 - 1)
                    nc.scalar.copy(xn1_t[:, t1 % 2, :, :], ps[:, 2, :].rearrange("p (c n) -> p c n", c=KC))\
                        .then_inc(xn1t_ready, 1)
                if s < TILES:
                    sqrt(1, s)
                    act.wait_ge(scaled[1], s + 1)
                    if s >= 2:
                        act.wait_ge(x1_ready, s - 1)
                    normalise(1, s, z1[:, s % 2, :], ps[:, s % 2, :], z1_ready)
                if 0 <= t2 < TILES:
                    sqrt(3, t2)
                if s < TILES:
                    sqrt(2, s)
                if 0 <= t2 < TILES:
                    act.wait_ge(scaled[3], t2 + 1)
                    if t2 >= 2:
                        act.wait_ge(out_ready, t2 - 1)
                    normalise(3, t2, z2[:, t2 % 2, :], y_sb[:, t2 % 2, :], z2_ready)
                if 0 <= t1 < TILES:
                    bring_table(0, t1)
                    act.wait_ge(gap_ready, t1 + 1)
                    nc.scalar.activation(gate[:, t1 % 2, 1:2], gate[:, t1 % 2, 0:1], ACT.Exp).then_inc(gexp_ready, 1)
                    bring_table(1, t1)

            for n in range(STEPS):
                u = n - ST_LAG
                if 0 <= u < UNITS:
                    act.wait_ge(t_psum, u + 1)
                    if u == 0:
                        act.wait_ge(proj_psum, len(SETS))
                        act.wait_ge(v_psum, 2)
                    if u == 2:
                        act.wait_ge(rot_r, len(SETS))
                        act.wait_ge(rot_i, len(SETS))
                    if u == 5:
                        act.wait_ge(part_l[0], len(SETS))
                        act.wait_ge(part_l[1], len(SETS))
                    if u >= PRING:
                        act.wait_ge(o_psum, 2 * ((u - PRING) // 4 + 1))
                    nc.scalar.activation(probs[:, u % PRING, :, :], ps[:, 3:6, :], ACT.Exp,
                                         scale=float(HEAD_DIM) ** -0.5).then_inc(exp_done, 1)
                gi, r = divmod(n - MAX_LAG, 4)
                if r == 0 and 0 <= gi < GROUPS:
                    act.wait_ge(mt_psum, gi + 1)
                    if gi >= 2:
                        act.wait_ge(mrow_stacked[gi % 2], 16 * (gi // 2))
                    nc.scalar.copy(mrow[0:PARTS * GROUP_HEADS, gi % 2, :],
                                   ps[0:PARTS * GROUP_HEADS, 0, 0:P].bitcast(BF16)).then_inc(mrow_ready, 1)
                gi, r = divmod(n - PV_LAG, 4)
                if r in (0, 2) and 0 <= gi < GROUPS:
                    qt = r // 2
                    act.wait_ge(o_psum, 2 * gi + qt + 1)
                    if gi >= 2 and qt == 0:
                        act.wait_ge(o_stored[gi % 2], 16 * (gi // 2))
                    nc.scalar.copy(o_sb[:, gi % 2, :, qt * P:(qt + 1) * P],
                                   ps[:, 6 + qt, :].rearrange("p (r n) -> p r n", r=REP)).then_inc(o_ready, 1)
                if n == MAX_LAG:
                    split_high(4)
                if n == MAX_LAG + 1:
                    split_middle(4)
                if n in EARLY:
                    tile_step(EARLY[n])
            for s in range(1, TILES + 2):
                tile_step(s)

        @block.vector
        def _(dve):
            chained = [0]

            def link(*instructions):
                for ins in instructions:
                    ins.then_inc(dve_chain, 1)
                chained[0] += len(instructions)
                dve.wait_ge(dve_chain, chained[0])

            def ln_stats(k, t, src):
                link(nc.vector.bn_stats(stats[:, k, t, :], src))
                nc.vector.bn_aggr(mv[:, k, t, :], stats[:, k, t, :]).then_inc(var_ready[k], 1)

            def ln_scale(k, t):
                dve.wait_ge(std_ready[k], t + 1)
                link(nc.vector.reciprocal(rstd[:, k, t:t + 1], std[:, k, t:t + 1]))
                nc.vector.scalar_tensor_tensor(out=nmr[:, k, t:t + 1], in0=mv[:, k, t, 0:1], scalar=-1.0,
                                               in1=rstd[:, k, t:t + 1], op0=ALU.mult, op1=ALU.mult)\
                    .then_inc(scaled[k], 1)

            def ln_apply(k, t, dst, src):
                return nc.vector.tensor_scalar(dst, src, mv[:, k, t, 0:1], rstd[:, k, t:t + 1],
                                               ALU.subtract, ALU.mult)

            def input_norm(t):
                ln_scale(0, t)
                ln_apply(0, t, xn_sb[:, t, :], x_sb[:, t, :]).then_inc(xn_ready, 1)

            for t in range(TILES):
                dve.wait_ge(x_loaded[t], 16)
                ln_stats(0, t, x_sb[:, t, :])
                if t >= 1:
                    input_norm(t - 1)
            input_norm(TILES - 1)

            dve.wait_ge(ident_loaded, 16)
            dve.wait_ge(mask_loaded, 16)
            nc.vector.tensor_copy(ident_bf[:, :], ident_sb[:, :]).then_inc(bf_const, 1)
            nc.vector.tensor_copy(mask_bf[:, :, :], mask_f[:, :].unsqueeze(1).broadcast_to([P, REP, P]))\
                .then_inc(bf_const, 1)
            dve.wait_ge(tab_loaded, 16)

            def rope(i, step):
                a = i % 2
                if step == 0:
                    tab = 2 if SETS[i] == "K" else 0
                    cos, sin = (tab_sb[:, tab + j, :].unsqueeze(1).broadcast_to([P, 2, SEQ]) for j in range(2))
                    re, im = (ps[:, bank, :].rearrange("p (b n) -> p b n", b=2) for bank in SET_BANKS[i])
                    dve.wait_ge(proj_psum, i + 1)
                    if i >= 2:
                        dve.wait_ge(rot_r, i - 1)
                        dve.wait_ge(rot_i, i - 1)
                    for j, (val, table) in enumerate(((re, cos), (im, sin), (re, sin), (im, cos))):
                        last = nc.vector.tensor_tensor(rope_t[:, a, j, :].rearrange("p (b n) -> p b n", b=2), val,
                                                       table, ALU.mult)
                    last.then_inc(rope_mul, 1)
                elif step == 1:
                    dve.wait_ge(rope_mul, i + 1)
                    if i >= 2:
                        dve.wait_ge(part_l[0], i - 1)
                    nc.vector.tensor_tensor(rot[:, a, 0, :], rope_t[:, a, 0, :], rope_t[:, a, 1, :], ALU.subtract)\
                        .then_inc(rot_r, 1)
                    dve.wait_ge(part_h, 2 * i + 1)
                    nc.vector.tensor_tensor(resid[:, a, 0, :], rot[:, a, 0, :], parts[:, a, 0, 0, :], ALU.subtract)\
                        .then_inc(resid1[0], 1)
                else:
                    dve.wait_ge(resid1[0], i + 1)
                    dve.wait_ge(part_m, 2 * i + 1)
                    nc.vector.tensor_tensor(parts[:, a, 0, 2, :], resid[:, a, 0, :], parts[:, a, 0, 1, :],
                                            ALU.subtract).then_inc(part_l[0], 1)

            for i in range(3):
                for step in range(3):
                    rope(i, step)
            rope(3, 0)

            def invert(gi):
                rows = slice(64 * (gi % 2), 64 * (gi % 2) + 64)
                dve.wait_ge(den_loaded[gi % 4], 16 * (gi // 4 + 1))
                if gi >= 2:
                    dve.wait_ge(rden_stored[gi % 2], 16 * (gi // 2))
                nc.vector.reciprocal(rden_pk[rows, :], den_pk[rows, :]).then_inc(rden_ready, 1)

            def gating_choice(t):
                ga = gate[:, t % 2, :]
                logits = ps[:, 5 + 2 * (t % 2), YB + EXPERTS * RANK:CATH]
                dve.wait_ge(cat_psum, t + 1)
                link(nc.vector.tensor_copy(ga[:, 48:56], logits))
                link(nc.vector.max(ga[:, 8:16], ga[:, 48:56]))
                nc.vector.tensor_tensor(ga[:, 0:1], ga[:, 9:10], ga[:, 8:9], ALU.subtract).then_inc(gap_ready, 1)
                link(nc.vector.max_index(gate_i[:, t % 2, :], ga[:, 8:16], ga[:, 48:56]))
                link(nc.vector.tensor_copy(ga[:, 16:18], gate_i[:, t % 2, 0:2]))

            def gating_weights(t):
                ga = gate[:, t % 2, :]
                dve.wait_ge(gexp_ready, t + 1)
                link(nc.vector.tensor_scalar(ga[:, 2:3], ga[:, 1:2], 1.0, None, ALU.add))
                link(nc.vector.reciprocal(ga[:, 3:4], ga[:, 2:3]))
                link(nc.vector.tensor_tensor(ga[:, 4:5], ga[:, 1:2], ga[:, 3:4], ALU.mult),
                     nc.vector.tensor_scalar(ga[:, 24:32], iota_sb[:, :], ga[:, 16:17], ga[:, 3:4],
                                             ALU.is_equal, ALU.mult))
                link(nc.vector.tensor_scalar(ga[:, 32:40], iota_sb[:, :], ga[:, 17:18], ga[:, 4:5],
                                             ALU.is_equal, ALU.mult))
                link(nc.vector.tensor_tensor(ga[:, 40:48], ga[:, 24:32], ga[:, 32:40], ALU.add))
                if t >= 2:
                    dve.wait_ge(hwt_psum, t - 1)
                down = ps[:, 5 + 2 * (t % 2), YB:YB + EXPERTS * RANK]
                nc.vector.tensor_tensor(hw[:, t % 2, :].rearrange("p (e r) -> p e r", r=RANK),
                                        down.rearrange("p (e r) -> p e r", r=RANK),
                                        ga[:, 40:48].unsqueeze(2).broadcast_to([P, EXPERTS, RANK]), ALU.mult)\
                    .then_inc(hw_ready, 1)

            def tile_step(s):
                t1, t2 = s - 1, s - 2
                if s < TILES:
                    dve.wait_ge(wo_psum, s + 1)
                    ln_stats(1, s, ps[:, s % 2, :])
                    ln_scale(1, s)
                if 0 <= t2 < TILES:
                    xb = 4 + 2 * (t2 % 2)
                    dve.wait_ge(y_psum, t2 + 1)
                    if t2 >= 2:
                        dve.wait_ge(z2_ready, t2 - 1)
                    nc.vector.tensor_tensor(y_sb[:, t2 % 2, 0:CATH], ps[:, xb, 0:CATH], bias_sb[:, 0:CATH], ALU.add)
                    nc.vector.tensor_tensor(y_sb[:, t2 % 2, CATH:DIM], ps[:, xb + 1, 0:YB], bias_sb[:, CATH:DIM],
                                            ALU.add).then_inc(y_ready, 1)
                    dve.wait_ge(y_ready, t2 + 1)
                    ln_stats(3, t2, y_sb[:, t2 % 2, :])
                if s < TILES:
                    dve.wait_ge(x1_ready, s + 1)
                    ln_stats(2, s, x_sb[:, s, :])
                if 0 <= t2 < TILES:
                    ln_scale(3, t2)
                if s < TILES:
                    ln_scale(2, s)
                    if s >= 2:
                        dve.wait_ge(xn1t_psum, s - 1)
                    ln_apply(2, s, xn1_sb[:, s % 2, :], x_sb[:, s, :]).then_inc(xn1_ready, 1)
                if 0 <= t1 < TILES:
                    gating_choice(t1)
                    gating_weights(t1)

            for n in range(STEPS):
                gi, k = divmod(n, GROUP_KV)
                if n < UNITS:
                    heads = slice(k * REP, (k + 1) * REP)
                    dve.wait_ge(s0_psum, n + 1)
                    nc.vector.tensor_reduce(nmax[:, gi % 2, 0, heads], ps[:, 0, :].rearrange("p (r k) -> p r k", r=REP),
                                            AX.X, ALU.max, negate=True).then_inc(s0_free, 1)
                    dve.wait_ge(s12_psum, n + 1)
                    nc.vector.tensor_reduce(nmax[:, gi % 2, 1, heads],
                                            ps[:, 1:3, :].rearrange("p a (r k) -> p r a k", r=REP),
                                            AX.XY, ALU.max, negate=True).then_inc(s12_free, 1)
                if k == 0 and 1 <= gi <= GROUPS:
                    full, left = nmax[:, (gi - 1) % 2, :, :], nmax_r[:, (gi - 1) % 2, :, :]
                    high, mid, low = (nmax_p[:, :, j, :] for j in range(PARTS))
                    dve.wait_ge(s12_free, n)
                    if gi >= 2:
                        dve.wait_ge(mt_psum, gi - 1)
                    link(nc.vector.tensor_copy(high, full))
                    link(nc.vector.tensor_tensor(left, full, high, ALU.subtract))
                    link(nc.vector.tensor_copy(mid, left))
                    nc.vector.tensor_tensor(low, left, mid, ALU.subtract).then_inc(nmax_split, 1)
                if n in LATE_ROPE:
                    rope(*LATE_ROPE[n])
                gi, r = divmod(n - PV_LAG - 6, 4)
                if r == 0 and 0 <= gi < GROUPS - 1:
                    invert(gi)
                if n in EARLY:
                    dve.wait_ge(late_loaded, 80)
                    tile_step(EARLY[n])
            for s in range(1, TILES + 2):
                tile_step(s)
                if s == 2:
                    invert(GROUPS - 1)

        @block.tensor
        def _(pe):
            pe.wait_ge(ident_loaded, 16)

            def turn_x(t):
                pe.wait_ge(xn_ready, t + 1)
                if t >= 2:
                    pe.wait_ge(xnt_ready, t - 1)
                for c in range(KC):
                    last = nc.tensor.transpose(ps[:, t % 2, c * P:(c + 1) * P], xn_sb[:, t, c * P:(c + 1) * P],
                                               ident_sb[:, :])
                last.then_inc(xnt_psum, 1)

            def project(i, first=0, count=2 * KC):
                if i >= 3:
                    pe.wait_ge(rope_mul, i - 2)
                if SETS[i] == "K":
                    pe.wait_ge(wk_loaded, 16)
                    pe.wait_ge(xnt_ready, TILES)
                    for ri in range(2):
                        for c in range(KC):
                            for half in range(2):
                                last = nc.tensor.matmul(ps[64 * half:64 * half + 64, SET_BANKS[i][ri], :],
                                                        wk_sb[:, c, 64 * ri:64 * ri + 64],
                                                        xn_t[:, c, half * HALF:(half + 1) * HALF],
                                                        start=(c == 0), stop=(c == KC - 1))
                else:
                    half, g = SETS[i]
                    pe.wait_ge(wq_loaded[g], 16)
                    if i == 2:
                        pe.wait_ge(v_ready, 2)
                    pe.wait_ge(xnt_ready, 4 * half + 4)
                    for m in range(first, first + count):
                        ri, c = divmod(m, KC)
                        col = (2 * g + ri) * P
                        last = nc.tensor.matmul(ps[:, SET_BANKS[i][ri], :], wq_sb[:, c, col:col + P],
                                                xn_t[:, c, half * HALF:(half + 1) * HALF],
                                                start=(c == 0), stop=(c == KC - 1))
                if first + count == 2 * KC:
                    last.then_inc(proj_psum, 1)

            def project_v(t):
                pe.wait_ge(wv_loaded, 16)
                pe.wait_ge(xnt_ready, t + 1)
                for c in range(KC):
                    last = nc.tensor.matmul(ps[:, 6 + t // 4, (t % 4) * P:(t % 4 + 1) * P],
                                            xn_t[:, c, t * P:(t + 1) * P], wv_sb[:, c, :],
                                            start=(c == 0), stop=(c == KC - 1))
                if t % 4 == 3:
                    last.then_inc(v_psum, 1)

            def turn_and_project_v(first):
                for t in range(first, first + 4):
                    turn_x(t)
                    if t > first:
                        project_v(t - 1)
                project_v(first + 3)

            turn_and_project_v(0)
            project(0)
            turn_and_project_v(4)
            for i in range(1, 4):
                project(i)

            def scores(n):
                gi, k = divmod(n, GROUP_KV)
                slot = gi % RING
                if k == 0:
                    pe.wait_ge(qk_loaded[slot], 32 * (gi // RING + 1))
                if n == 0:
                    pe.wait_ge(bf_const, 2)
                    pe.wait_ge(v_ready, 2)
                    pe.wait_ge(rope_mul, 4)
                    pe.wait_ge(pool_const, 4)
                else:
                    pe.wait_ge(s0_free, n)
                gj, r = divmod(n - MAX_LAG - 1, 4)
                if r == 0 and 0 <= gj < GROUPS:
                    pe.wait_ge(mrow_ready, gj + 1)
                nc.tensor.matmul(ps[:, 0, :], ident_bf[:, :], mask_bf[:, :, :].rearrange("p r k -> p (r k)"),
                                 start=True, stop=False, skip_group_check=True)
                for r in range(REP):
                    h = k * REP + r
                    last = nc.tensor.matmul(ps[:, 0, r * P:(r + 1) * P], qst[0:SROWS, slot, h, 0:P],
                                            kst[0:SROWS, slot, k, 0:P], start=False, stop=(r == REP - 1),
                                            skip_group_check=True)
                last.then_inc(s0_psum, 1)

            def scores_more(n):
                gi, k = divmod(n, GROUP_KV)
                slot = gi % RING
                if n >= 1:
                    pe.wait_ge(s12_free, n)
                nc.tensor.matmul(ps[:, 2, :], ident_bf[:, :], mask_bf[:, :, :].rearrange("p r k -> p (r k)"),
                                 start=True, stop=False, skip_group_check=True)
                for r in range(REP):
                    h = k * REP + r
                    for kt in range(2):
                        last = nc.tensor.matmul(ps[:, 1 + kt, r * P:(r + 1) * P], qst[0:SROWS, slot, h, P:2 * P],
                                                kst[0:SROWS, slot, k, kt * P:(kt + 1) * P], start=(kt == 0),
                                                stop=(r == REP - 1), skip_group_check=True)
                last.then_inc(s12_psum, 1)

            def turn_max(gi, n):
                pe.wait_ge(nmax_split, gi + 1)
                pe.wait_ge(s0_free, min(n + 1, UNITS))
                for qt in range(2):
                    last = nc.tensor.transpose(ps[0:PARTS * GROUP_HEADS, 0, qt * 64:(qt + 1) * 64].bitcast(BF16),
                                               nmax_p[:, qt, :, :].rearrange("p a h -> p (a h)"), ident_bf[:, :])
                last.then_inc(mt_psum, 1)

            def scores_t(u):
                gi, k = divmod(u, GROUP_KV)
                slot = gi % RING
                if k == 0:
                    pe.wait_ge(mrow_stacked[gi % 2], 16 * (gi // 2 + 1))
                if u == 0:
                    pe.wait_ge(rope_mul, 5)
                else:
                    pe.wait_ge(exp_done, u)
                for j, (kt, qt) in enumerate(((0, 0), (0, 1), (1, 1))):
                    last = nc.tensor.matmul(ps[:, 3 + j, :], kst[0:TROWS, slot, k, kt * P:(kt + 1) * P],
                                            qst[0:TROWS, slot, k * REP:(k + 1) * REP, qt * P:(qt + 1) * P],
                                            start=True, stop=True)
                last.then_inc(t_psum, 1)

            def attend(gi, piece):
                b, g = divmod(gi, 2)
                qt, kt = ((0, 0), (1, 0), (1, 1))[piece]
                pe.wait_ge(probs_masked, 4 * gi + 4)
                if gi >= 1 and kt == 0:
                    pe.wait_ge(o_ready, 2 * gi - 1 + qt)
                for j in range(GROUP_KV):
                    u = gi * GROUP_KV + j
                    last = nc.tensor.matmul(ps[32 * j:32 * j + 32, 6 + qt, :],
                                            v_aug[:, 2 * b + kt, g * GROUP_KV + j, :],
                                            probs[:, u % PRING, qt + kt, :],
                                            start=(kt == 0), stop=(kt == qt))
                if kt == qt:
                    last.then_inc(o_psum, 1)

            def project_out(t):
                if t == 0:
                    pe.wait_ge(late_loaded, 80)
                    pe.wait_ge(s12_free, UNITS)
                    pe.wait_ge(mrow_ready, GROUPS)
                pe.wait_ge(attn_ready, t // 2 + 1)
                if t >= 2:
                    pe.wait_ge(z1_ready, t - 1)
                for r in range(REP):
                    col = r * SEQ + (t % 2) * P
                    last = nc.tensor.matmul(ps[:, t % 2, :], attn_t[:, t // 2, col:col + P], wo_sb[:, r, :],
                                            start=(r == 0), stop=(r == REP - 1))
                last.then_inc(wo_psum, 1)

            def turn_mid(t):
                pe.wait_ge(xn1_ready, t + 1)
                if t >= 1:
                    pe.wait_ge(xn1t_ready, t)
                for c in range(KC):
                    last = nc.tensor.transpose(ps[:, 2, c * P:(c + 1) * P], xn1_sb[:, t % 2, c * P:(c + 1) * P],
                                               ident_sb[:, :])
                last.then_inc(xn1t_psum, 1)

            def base_down_router(t):
                pe.wait_ge(xn1t_ready, t + 1)
                if t >= 2:
                    pe.wait_ge(y_ready, t - 1)
                if t == 1:
                    pe.wait_ge(o_ready, 2 * GROUPS)
                for hf in range(2):
                    for c in range(KC):
                        last = nc.tensor.matmul(ps[:, 4 + 2 * (t % 2) + hf, 0:CATH], xn1_t[:, t % 2, c, :],
                                                wcat_sb[:, c, hf * CATH:(hf + 1) * CATH],
                                                start=(c == 0), stop=(hf == 1 and c == KC - 1),
                                                skip_group_check=True)
                last.then_inc(cat_psum, 1)

            def turn_hw(t):
                pe.wait_ge(hw_ready, t + 1)
                if t >= 1:
                    pe.wait_ge(hwt_ready, t)
                nc.tensor.transpose(ps[:, 3, 0:P], hw[:, t % 2, :], ident_sb[:, :]).then_inc(hwt_psum, 1)

            def up_projection(t):
                pe.wait_ge(hwt_ready, t + 1)
                nc.tensor.matmul(ps[:, 4 + 2 * (t % 2), 0:CATH], hw_t[:, t % 2, :], lora_b_sb[:, 0:CATH],
                                 start=False, stop=True, skip_group_check=True)
                nc.tensor.matmul(ps[:, 5 + 2 * (t % 2), 0:YB], hw_t[:, t % 2, :], lora_b_sb[:, CATH:DIM],
                                 start=False, stop=True, skip_group_check=True).then_inc(y_psum, 1)

            def tile_step(s):
                if 2 <= s < TILES:
                    project_out(s)
                if 0 <= s - 2 < TILES:
                    turn_hw(s - 2)
                if 0 <= s - 1 < TILES:
                    turn_mid(s - 1)
                if 0 <= s - 2 < TILES:
                    up_projection(s - 2)
                if s == 1:
                    pe.wait_ge(exp_done, UNITS)
                if 0 <= s - 1 < TILES:
                    base_down_router(s - 1)

            for n in range(STEPS):
                if n < UNITS:
                    scores(n)
                if 0 <= n - ST_LAG < UNITS:
                    scores_t(n - ST_LAG)
                if n < UNITS:
                    scores_more(n)
                if n < 4:
                    project(4, 2 * n, 2)
                gi, r = divmod(n - MAX_LAG, 4)
                if r == 0 and 0 <= gi < GROUPS:
                    turn_max(gi, n)
                gi, r = divmod(n - PV_LAG, 4)
                if r < 3 and 0 <= gi < GROUPS:
                    attend(gi, r)
                if n in EARLY_OUT:
                    project_out(EARLY_OUT[n])
            for s in range(1, TILES + 2):
                tile_step(s)


def rotary_tables():
    freqs = 1.0 / np.float32(10000.0) ** (np.arange(0, HEAD_DIM, 2, dtype=np.float32) / HEAD_DIM)
    angles = (np.arange(SEQ, dtype=np.float32)[:, None] * freqs.astype(np.float32)[None]).astype(np.float32)
    rows_q = np.arange(P) // GROUP_HEADS
    rows_k = (np.arange(P) % 64) // KV_HEADS
    return np.stack([f(angles).T[rows] for rows in (rows_q, rows_k) for f in (np.cos, np.sin)], axis=1)\
        .astype(np.float32)


def kernel(L0_attn_x, L0_attn_wq, L0_attn_wk, L0_attn_wv, L0_attn_wo, L0_ffn_W_base, L0_ffn_b_base, L0_ffn_W_gate,
           L0_ffn_A, L0_ffn_B):
    from concourse import bacc
    from concourse.bass_utils import run_bass_kernel_spmd

    def arr(a):
        return np.asarray(a)

    wq = arr(L0_attn_wq).reshape(DIM, 2, GROUP_HEADS, FREQS, 2).transpose(0, 1, 4, 3, 2).reshape(DIM, DIM)
    wk = arr(L0_attn_wk).reshape(DIM, KV_HEADS, FREQS, 2).transpose(0, 3, 2, 1).reshape(DIM, P)
    wo = arr(L0_attn_wo).reshape(KV_HEADS, REP, HEAD_DIM, DIM).transpose(1, 0, 2, 3).reshape(DIM, DIM)
    wcat = np.concatenate([arr(L0_ffn_W_base).T, arr(L0_ffn_A).reshape(EXPERTS * RANK, DIM).T,
                           arr(L0_ffn_W_gate).T], axis=1)
    lora_b = arr(L0_ffn_B).transpose(0, 2, 1).reshape(EXPERTS * RANK, DIM)
    later = np.arange(P)[None, :] > np.arange(P)[:, None]
    arrays = {
        "x": arr(L0_attn_x).reshape(TOKENS, DIM), "wq": wq, "wk": wk, "wv": arr(L0_attn_wv), "wo": wo,
        "wcat": wcat, "lora_b": lora_b, "bias": arr(L0_ffn_b_base), "tables": rotary_tables(),
        "ident": np.eye(P, dtype=np.float32), "maskq": np.where(later, np.float32(MASKED), np.float32(0)),
        "iota": np.tile(np.arange(EXPERTS, dtype=np.float32), (P, 1)),
    }
    arrays = {n: np.ascontiguousarray(a) for n, a in arrays.items()}
    nc = bacc.Bacc("TRN2", target_bir_lowering=False, num_devices=1)
    args = [nc.dram_tensor(n, a.shape, mybir.dt.from_np(a.dtype), kind="ExternalInput").ap() for n, a in arrays.items()]
    out = nc.dram_tensor("out", [TOKENS, DIM], F32, kind="ExternalOutput").ap()
    build(nc, *args, out)
    r = run_bass_kernel_spmd(nc, [arrays], core_ids=[0])
    return r.results[0]["out"].reshape(BATCH, SEQ, DIM)
```

```python
from contextlib import ExitStack

import numpy as np

import concourse.bass as bass
from concourse import mybir

F32 = mybir.dt.float32
F32R = mybir.dt.float32r
BF16 = mybir.dt.bfloat16
U32 = mybir.dt.uint32
ALU = mybir.AluOpType
ACT = mybir.ActivationFunctionType
AX = mybir.AxisListType

P = 128
BATCH, SEQ, DIM = 4, 256, 512
HEADS, KV_HEADS, HEAD_DIM = 32, 8, 16
REP = HEADS // KV_HEADS
FREQS = HEAD_DIM // 2
EXPERTS, RANK = 8, 16
EPS = 1e-5
TOKENS = BATCH * SEQ
TILES = TOKENS // P
KC = DIM // P
HALF = TOKENS // 2
GROUP_KV = 4
GROUP_HEADS = GROUP_KV * REP
GROUPS = BATCH * KV_HEADS // GROUP_KV
UNITS = BATCH * KV_HEADS
PARTS = 3
RUNS = ((0, 3), (3, 2), (5, 1))
TERMS = 6
SROWS = TERMS * HEAD_DIM
TROWS = SROWS + PARTS
RING = 4
PRING = 8
ST_LAG = 7
MAX_LAG = 5
PV_LAG = 12
STEPS = 4 * (GROUPS - 1) + PV_LAG + 3
VECTOR_OUT = 5
EARLY = {UNITS + ST_LAG - 1: 0, STEPS - 2: 1}
EARLY_OUT = {UNITS + 1: 0, UNITS + ST_LAG - 1: 1}
ROPE_3 = {0: 1, 1: 2}
MATMULS_4 = (1, 1, 1, 1, 1)
ROTATE_4, SPLIT_HIGH_4, SPLIT_MIDDLE_4, WRITE_4 = 5, 10, 12, 14
SPLIT_WEIGHTS = {15 + j: j for j in range(8)}
CAT = DIM + EXPERTS * RANK + EXPERTS
CATH = CAT // 2
YB = DIM - CATH
MASKED = -(2.0 ** 127)


def build(nc, x, wq, wk, wv, wo, wcat, lora_b, bias, tables, ident, maskq, iota, out):
    ctx = ExitStack()
    with ctx:
        place = {}

        def sb(name, shape, dt=F32):
            place[name] = nc.sbuf_base
            return ctx.enter_context(nc.sbuf_tensor(name, shape, dt))

        def over(name, shape, region, column):
            return nc.alloc_sbuf_tensor_at(name, shape, F32R, offset=place[region] + 4 * column)

        def sem(name):
            return ctx.enter_context(nc.semaphore(name))

        x_sb = sb("x_sb", [P, TILES, DIM])
        region_c = sb("region_c", [P, 7168])
        wq_sb = region_c[:, 0:2048].rearrange("p (c n) -> p c n", c=KC)
        wk_sb = region_c[:, 2048:2560].rearrange("p (c n) -> p c n", c=KC)
        wv_sb = region_c[:, 2560:3072].rearrange("p (c n) -> p c n", c=KC)
        tab_sb = region_c[:, 3072:4096].rearrange("p (a n) -> p a n", a=4)
        parts = region_c[:, 4096:7168].bitcast(BF16).rearrange("p (a i s n) -> p a i s n", a=2, i=2, s=PARTS)
        wo_h = over("wo_h", [P, REP, DIM], "region_c", 0)
        attn_h = over("attn_h", [P, 2, REP * SEQ], "region_c", 2048)
        wcat_h = over("wcat_h", [P, KC, CAT], "region_c", 4096)
        wo_sb = sb("wo_sb", [P, REP, DIM])
        wcat_sb = sb("wcat_sb", [P, KC, CAT])
        wo_l = over("wo_l", [P, REP, DIM], "wo_sb", 0)
        wcat_l = over("wcat_l", [P, KC, CAT], "wcat_sb", 0)
        lora_b_sb = sb("lora_b_sb", [P, DIM])
        bias_sb = sb("bias_sb", [P, DIM])
        ident_sb = sb("ident_sb", [P, P])
        ident_bf = sb("ident_bf", [P, P], BF16)
        mask_f = sb("mask_f", [P, P])
        mask_bf = sb("mask_bf", [P, REP, P], BF16)
        iota_sb = sb("iota_sb", [P, EXPERTS])
        eps_sb = sb("eps_sb", [P, 1])
        kst = sb("kst", [P, RING, GROUP_KV, SEQ], BF16)
        v_aug = sb("v_aug", [P, TILES, KV_HEADS, 32])
        o_sb = sb("o_sb", [P, 2, REP, SEQ])
        attn_t = sb("attn_t", [P, BATCH, REP * SEQ])
        attn_l = over("attn_l", [P, BATCH, REP * SEQ], "attn_t", 0)
        late_set = region_c[:, 2048:3072].rearrange("p (i n) -> p i n", i=2)
        late_mul = attn_t[:, 2:4, :].rearrange("p b (j n) -> p (b j) n", j=2)
        late_rot = attn_t[:, 1, :].rearrange("p (i n) -> p i n", i=2)
        late_resid = [late_mul[:, 0, :], late_mul[:, 2, :]]
        rden_bc = sb("rden_bc", [P, REP * SEQ])
        den_pk = sb("den_pk", [P, 64])
        rden_pk = sb("rden_pk", [P, 64])
        nmax = sb("nmax", [P, 2, 2, GROUP_HEADS])
        nmax_r = sb("nmax_r", [P, 2, 2, GROUP_HEADS])
        nmax_p = sb("nmax_p", [P, 2, PARTS, GROUP_HEADS], BF16)
        mrow = sb("mrow", [P, 2, SEQ], BF16)
        stats = sb("stats", [P, 4, TILES, 6])
        mv = sb("mv", [P, 4, TILES, 2])
        std = sb("std", [P, 4, TILES])
        rstd = sb("rstd", [P, 4, TILES])
        nmr = sb("nmr", [P, 4, TILES])
        unused = sb("unused", [P, 2, TILES + 1])
        gate = sb("gate", [P, 2, 64])
        gate_i = sb("gate_i", [P, 2, 8], U32)
        region_a = sb("region_a", [P, 12 * 1024])
        xn_t = region_a[:, 0:4096].rearrange("p (c n) -> p c n", c=KC)
        rope_t = region_a[:, 4096:8192].rearrange("p (a b n) -> p a b n", a=2, b=4)
        rot = region_a[:, 8192:10240].rearrange("p (a b n) -> p a b n", a=2, b=2)
        resid = region_a[:, 10240:12288].rearrange("p (a b n) -> p a b n", a=2, b=2)
        probs = region_a[:, :].rearrange("p (u a n) -> p u a n", u=PRING, a=3)
        region_b = sb("region_b", [P, 8192])
        qst = region_b[:, :].bitcast(BF16).rearrange("p (s h n) -> p s h n", s=RING, h=GROUP_HEADS)
        xn_sb = region_b[:, 4096:8192].rearrange("p (t n) -> p t n", t=TILES)
        z1 = region_b[:, 0:1024].rearrange("p (a n) -> p a n", a=2)
        xn1_sb = region_b[:, 1024:2048].rearrange("p (a n) -> p a n", a=2)
        hw = region_b[:, 2048:2304].rearrange("p (a n) -> p a n", a=2)
        hw_t = region_b[:, 2304:2560].rearrange("p (a n) -> p a n", a=2)
        xn1_h = over("xn1_h", [P, 2, KC, P], "region_b", 2560)
        xn1_l = over("xn1_l", [P, 2, KC, P], "region_b", 6656)
        y_sb = region_b[:, 3584:4608].rearrange("p (a n) -> p a n", a=2)
        z2 = region_b[:, 4608:5632].rearrange("p (a n) -> p a n", a=2)
        out_sb = region_b[:, 5632:6656].rearrange("p (a n) -> p a n", a=2)

        ps = ctx.enter_context(nc.psum_tensor("ps", [P, 8, 512], F32))

        q_scr = nc.dram_tensor("q_scr", [2, SROWS, GROUP_HEADS, TOKENS], BF16, kind="Internal").ap()
        k_scr = nc.dram_tensor("k_scr", [2, SROWS, KV_HEADS, HALF], BF16, kind="Internal").ap()
        o_scr = nc.dram_tensor("o_scr", [GROUPS, P, REP * SEQ], F32, kind="Internal").ap()
        r_scr = nc.dram_tensor("r_scr", [GROUPS, 64, 64], F32, kind="Internal").ap()

        x_loaded = [sem(f"x_loaded{t}") for t in range(TILES)]
        ident_loaded = sem("ident_loaded")
        mask_loaded = sem("mask_loaded")
        wq_loaded = [sem(f"wq_loaded{g}") for g in range(2)]
        tab_loaded = sem("tab_loaded")
        wk_loaded = sem("wk_loaded")
        wv_loaded = sem("wv_loaded")
        late_loaded = sem("late_loaded")
        dve_chain = sem("dve_chain")
        pool_const = sem("pool_const")
        bf_const = sem("bf_const")
        var_ready = [sem(f"var_ready{i}") for i in range(4)]
        std_ready = [sem(f"std_ready{i}") for i in range(4)]
        scaled = [sem(f"scaled{i}") for i in range(4)]
        xn_ready = sem("xn_ready")
        xnt_psum = sem("xnt_psum")
        xnt_ready = sem("xnt_ready")
        proj_psum = sem("proj_psum")
        v_psum = sem("v_psum")
        v_ready = sem("v_ready")
        rope_mul = sem("rope_mul")
        rot_r = sem("rot_r")
        rot_i = sem("rot_i")
        part_h = sem("part_h")
        resid1 = [sem("resid1_r"), sem("resid1_i")]
        part_m = sem("part_m")
        part_l = [sem("part_l_r"), sem("part_l_i")]
        late_copied = sem("late_copied")
        late_multiplied = sem("late_multiplied")
        late_rotated = sem("late_rotated")
        late_left = sem("late_left")
        late_low = sem("late_low")
        scr_written = [sem(f"scr_written{i}") for i in range(5)]
        k_written = [sem(f"k_written{i}") for i in range(2)]
        qk_loaded = [sem(f"qk_loaded{i}") for i in range(RING)]
        s0_psum = sem("s0_psum")
        s12_psum = sem("s12_psum")
        s0_free = sem("s0_free")
        s12_free = sem("s12_free")
        nmax_split = sem("nmax_split")
        mt_psum = sem("mt_psum")
        mrow_ready = sem("mrow_ready")
        mrow_stacked = [sem(f"mrow_stacked{i}") for i in range(2)]
        t_psum = sem("t_psum")
        exp_done = sem("exp_done")
        probs_masked = sem("probs_masked")
        o_psum = sem("o_psum")
        o_ready = [sem("o_ready_scalar"), sem("o_ready_vector")]
        o_stored = [sem(f"o_stored{i}") for i in range(2)]
        den_loaded = [sem(f"den_loaded{i}") for i in range(4)]
        num_loaded = [sem(f"num_loaded{i}") for i in range(4)]
        rden_ready = sem("rden_ready")
        rden_stored = [sem(f"rden_stored{i}") for i in range(2)]
        rden_loaded = [sem(f"rden_loaded{i}") for i in range(4)]
        attn_ready = sem("attn_ready")
        attn_high = sem("attn_high")
        attn_low = sem("attn_low")
        weight_high = sem("weight_high")
        weight_low = sem("weight_low")
        wo_psum = sem("wo_psum")
        z1_ready = sem("z1_ready")
        x1_ready = sem("x1_ready")
        xn1_ready = sem("xn1_ready")
        xn1t_psum = sem("xn1t_psum")
        xn1_high = sem("xn1_high")
        xn1_low = sem("xn1_low")
        cat_psum = sem("cat_psum")
        gap_ready = sem("gap_ready")
        gexp_ready = sem("gexp_ready")
        hw_ready = sem("hw_ready")
        hwt_psum = sem("hwt_psum")
        hwt_ready = sem("hwt_ready")
        y_psum = sem("y_psum")
        y_ready = sem("y_ready")
        z2_ready = sem("z2_ready")
        out_ready = sem("out_ready")
        last_ready = sem("last_ready")
        out_stored = [sem(f"out_stored{i}") for i in range(2)]

        SETS = [(0, 0), "K", (0, 1), (1, 0), (1, 1)]
        SET_BANKS = [(2, 3), (4, 5), (6, 7), (2, 3), (4, 5)]
        set_of = {s: i for i, s in enumerate(SETS)}
        WRITES_Q = WRITES_K = 16 * 2 * len(RUNS)

        quarters = [(w[:, j, :], h[:, j, :], l[:, j, :]) for w, h, l in ((wo_sb, wo_h, wo_l), (wcat_sb, wcat_h, wcat_l))
                    for j in range(4)]

        def wait_o(engine, count):
            late = count - 2 * VECTOR_OUT
            engine.wait_ge(o_ready[late > 0], late if late > 0 else count)

        def copy_o(engine, copy, gi, qt):
            engine.wait_ge(o_psum, 2 * gi + qt + 1)
            if gi >= 2 and qt == 0:
                engine.wait_ge(o_stored[gi % 2], 16 * (gi // 2))
            copy(o_sb[:, gi % 2, :, qt * P:(qt + 1) * P], ps[:, 6 + qt, :].rearrange("p (r n) -> p r n", r=REP))\
                .then_inc(o_ready[gi >= VECTOR_OUT], 1)

        block = ctx.enter_context(nc.Block())

        @block.sync
        def _(sp):
            sp.dma_start(x_sb[:, 0, :], x[0:P, :]).then_inc(x_loaded[0], 16)
            sp.dma_start(ident_sb[:, :], ident).then_inc(ident_loaded, 16)
            sp.dma_start(wv_sb[:, :, :], wv.rearrange("(c p) n -> p c n", p=P)).then_inc(wv_loaded, 16)
            wq_v = wq.rearrange("(c p) n -> p c n", p=P)
            for t in range(1, TILES):
                if t == 4:
                    sp.dma_start(wq_sb[:, :, 0:256], wq_v[:, :, 0:256]).then_inc(wq_loaded[0], 16)
                sp.dma_start(x_sb[:, t, :], x[t * P:(t + 1) * P, :]).then_inc(x_loaded[t], 16)
            sp.dma_start(tab_sb[:, :, :], tables).then_inc(tab_loaded, 16)
            sp.dma_start(wk_sb[:, :, :], wk.rearrange("(c p) n -> p c n", p=P)).then_inc(wk_loaded, 16)
            sp.dma_start(wq_sb[:, :, 256:512], wq_v[:, :, 256:512]).then_inc(wq_loaded[1], 16)
            sp.dma_start(mask_f[:, :], maskq).then_inc(mask_loaded, 16)
            sp.dma_start(wo_sb[:, :, :], wo.rearrange("(r p) n -> p r n", p=P)).then_inc(late_loaded, 16)
            sp.dma_start(wcat_sb[:, :, :], wcat.rearrange("(c p) n -> p c n", p=P)).then_inc(late_loaded, 16)
            sp.dma_start(lora_b_sb[:, :], lora_b).then_inc(late_loaded, 16)
            sp.dma_start(bias_sb[:, :], bias.partition_broadcast(P)).then_inc(late_loaded, 16)
            sp.dma_start(iota_sb[:, :], iota).then_inc(late_loaded, 16)

            def write_q(i):
                half, g = SETS[i]
                dst = q_scr[g].rearrange("(s i f) h n -> i (f h) s n", s=TERMS, i=2)
                for ri in range(2):
                    if i == 4:
                        sp.wait_ge(late_low, ri + 1)
                    else:
                        sp.wait_ge(part_l[ri], i + 1)
                    sp.wait_ge(part_m, 2 * i + 1 + ri)
                    for first, count in RUNS:
                        sp.dma_start(dst[ri, :, first:first + count, half * HALF:(half + 1) * HALF],
                                     parts[:, i % 2, ri, 0:count, :]).then_inc(scr_written[i], 16)

            def write_k(part, half):
                i = set_of["K"]
                first, count = RUNS[part]
                dst = k_scr[half].rearrange("(s i f) h n -> i (f h) s n", s=TERMS, i=2)
                for ri in range(2):
                    if part == 0:
                        sp.wait_ge(part_h, 2 * i + 1 + ri)
                    elif part == 1:
                        sp.wait_ge(part_m, 2 * i + 1 + ri)
                    else:
                        sp.wait_ge(part_l[ri], i + 1)
                    rows = parts[half * 64:half * 64 + 64, i % 2, ri, part:part + 1, :]
                    sp.dma_start(dst[ri, :, first:first + count, :], rows.broadcast_to([64, count, HALF]))\
                        .then_inc(k_written[half], 16)

            def wait_ring(gi):
                if gi >= RING:
                    sp.wait_ge(t_psum, 2 * GROUP_KV * (gi - RING + 1))
                elif gi >= 2:
                    sp.wait_ge(xnt_psum, TILES)

            def load_q(gi):
                b, g = divmod(gi, 2)
                sp.wait_ge(scr_written[set_of[b // 2, g]], WRITES_Q)
                wait_ring(gi)
                sp.dma_start(qst[0:SROWS, gi % RING, :, :], q_scr[g, :, :, b * SEQ:(b + 1) * SEQ])\
                    .then_inc(qk_loaded[gi % RING], 16)

            def load_k(gi):
                b, g = divmod(gi, 2)
                sp.wait_ge(k_written[b // 2], WRITES_K)
                wait_ring(gi)
                sp.dma_start(kst[0:SROWS, gi % RING, :, :],
                             k_scr[b // 2, :, g * GROUP_KV:(g + 1) * GROUP_KV, (b % 2) * SEQ:(b % 2 + 1) * SEQ])\
                    .then_inc(qk_loaded[gi % RING], 16)

            def stack_max(gi):
                sp.wait_ge(mrow_ready, gi + 1)
                sp.dma_start(qst[SROWS:TROWS, gi % RING, :, :], mrow[0:PARTS * GROUP_HEADS, gi % 2, :])\
                    .then_inc(mrow_stacked[gi % 2], 16)

            def send_out(gi):
                wait_o(sp, 2 * gi + 2)
                sp.dma_start(o_scr[gi], o_sb[:, gi % 2, :, :].rearrange("p r n -> p (r n)"))\
                    .then_inc(o_stored[gi % 2], 16)

            def fetch_out(gi):
                b, g = divmod(gi, 2)
                rows = slice(64 * g, 64 * g + 64)
                src = o_scr[gi].rearrange("(j e) n -> j e n", j=GROUP_KV)
                sp.wait_ge(o_stored[gi % 2], 16 * (gi // 2 + 1))
                if gi >= 2:
                    sp.wait_ge(rden_ready, gi - 1)
                sp.dma_start(den_pk[rows, :], src[:, HEAD_DIM, :].rearrange("j (c n) -> j c n", n=64))\
                    .then_inc(den_loaded[gi % 4], 16)
                sp.dma_start(attn_t[rows, b, :], src[:, 0:HEAD_DIM, :]).then_inc(num_loaded[gi % 4], 16)

            def store_rden(gi):
                sp.wait_ge(rden_ready, gi + 1)
                sp.dma_start(r_scr[gi], rden_pk[64 * (gi % 2):64 * (gi % 2) + 64, :]).then_inc(rden_stored[gi % 2], 16)

            def spread_rden(gi):
                b, g = divmod(gi, 2)
                sp.wait_ge(rden_stored[g], 16 * (b + 1))
                if b >= 1:
                    sp.wait_ge(attn_ready, b)
                src = r_scr[gi].rearrange("(j c) n -> j (c n)", j=GROUP_KV)
                sp.dma_start(rden_bc[64 * g:64 * g + 64, :],
                             src.unsqueeze(1).broadcast_to([GROUP_KV, HEAD_DIM, REP * SEQ]))\
                    .then_inc(rden_loaded[gi % 4], 16)

            write_q(0)
            load_q(0)
            load_q(2)
            for part in range(PARTS):
                for half in range(2):
                    write_k(part, half)
            load_k(0)
            load_k(1)
            write_q(2)
            load_q(1)
            load_k(2)
            load_k(3)
            load_q(3)
            write_q(3)
            for n in range(MAX_LAG, STEPS + 5):
                for lag, count, what in ((MAX_LAG, GROUPS, stack_max), (PV_LAG + 3, GROUPS, send_out),
                                         (PV_LAG + 4, GROUPS, fetch_out), (PV_LAG + 6, GROUPS, store_rden),
                                         (PV_LAG + 7, GROUPS, spread_rden)):
                    gi, r = divmod(n - lag, 4)
                    if r == 0 and 0 <= gi < count:
                        what(gi)
                if n == WRITE_4:
                    write_q(4)
                gi, r = divmod(n - ST_LAG - 4, 4)
                if r == 0 and 0 <= gi < GROUPS - RING:
                    load_k(gi + RING)
                    load_q(gi + RING)
            for t in range(TILES):
                if t < TILES - 1:
                    sp.wait_ge(out_ready, t + 1)
                else:
                    sp.wait_ge(last_ready, 1)
                sp.dma_start(out[t * P:(t + 1) * P, :], out_sb[:, t % 2, :]).then_inc(out_stored[t % 2], 16)
            for i in range(2):
                sp.wait_ge(out_stored[i], 16 * TILES // 2)

        @block.gpsimd
        def _(pool):
            pool.memset(eps_sb[:, :], EPS).then_inc(pool_const, 1)
            pool.memset(v_aug[:, :, :, :], 0.0).then_inc(pool_const, 1)
            pool.wait_ge(pool_const, 2)
            pool.memset(v_aug[:, :, :, HEAD_DIM:HEAD_DIM + 1], 1.0).then_inc(pool_const, 1)
            pool.wait_ge(pool_const, 3)
            pool.memset(kst[SROWS:TROWS, :, :, :], 1.0).then_inc(pool_const, 1)
            pool.wait_ge(pool_const, 4)
            for i in range(len(SETS) - 1):
                a = i % 2
                pool.wait_ge(rope_mul, i + 1)
                if i >= 2:
                    pool.wait_ge(part_l[1], i - 1)
                    pool.wait_ge(part_h, 2 * (i - 2) + 2)
                pool.tensor_tensor(rot[:, a, 1, :], rope_t[:, a, 2, :], rope_t[:, a, 3, :], ALU.add).then_inc(rot_i, 1)
                pool.wait_ge(rot_i, i + 1)
                pool.wait_ge(part_h, 2 * i + 2)
                pool.tensor_tensor(resid[:, a, 1, :], rot[:, a, 1, :], parts[:, a, 1, 0, :], ALU.subtract)\
                    .then_inc(resid1[1], 1)
                pool.wait_ge(resid1[1], i + 1)
                pool.wait_ge(part_m, 2 * i + 2)
                pool.tensor_tensor(parts[:, a, 1, 2, :], resid[:, a, 1, :], parts[:, a, 1, 1, :], ALU.subtract)\
                    .then_inc(part_l[1], 1)
            def rotate_late():
                cos, sin = (tab_sb[:, j, :].unsqueeze(1).broadcast_to([P, 2, SEQ]) for j in range(2))
                re, im = (late_set[:, i, :].rearrange("p (b n) -> p b n", b=2) for i in range(2))
                pool.wait_ge(late_copied, 2)
                for j, (val, table) in enumerate(((re, cos), (im, sin), (re, sin), (im, cos))):
                    pool.tensor_tensor(late_mul[:, j, :].rearrange("p (b n) -> p b n", b=2), val, table, ALU.mult)\
                        .then_inc(late_multiplied, 1)
                for i, op in enumerate((ALU.subtract, ALU.add)):
                    pool.wait_ge(late_multiplied, 2 * i + 2)
                    pool.tensor_tensor(late_rot[:, i, :], late_mul[:, 2 * i, :], late_mul[:, 2 * i + 1, :], op)\
                        .then_inc(late_rotated, 1)

            def leave_late():
                for i in range(2):
                    pool.wait_ge(late_rotated, i + 1)
                    pool.wait_ge(part_h, 2 * 4 + 1 + i)
                    pool.tensor_tensor(late_resid[i], late_rot[:, i, :], parts[:, 0, i, 0, :], ALU.subtract)\
                        .then_inc(late_left, 1)

            def low_late():
                for i in range(2):
                    pool.wait_ge(late_left, i + 1)
                    pool.wait_ge(part_m, 2 * 4 + 1 + i)
                    pool.tensor_tensor(parts[:, 0, i, 2, :], late_resid[i], parts[:, 0, i, 1, :], ALU.subtract)\
                        .then_inc(late_low, 1)

            def divide(b):
                for g in range(2):
                    pool.wait_ge(num_loaded[(2 * b + g) % 4], 16 * (b // 2 + 1))
                    pool.wait_ge(rden_loaded[(2 * b + g) % 4], 16 * (b // 2 + 1))
                pool.tensor_tensor(attn_t[:, b, :], attn_t[:, b, :], rden_bc[:, :], ALU.mult).then_inc(attn_ready, 1)

            def attn_low_part(b):
                pool.wait_ge(attn_high, b + 1)
                pool.tensor_tensor(attn_l[:, b, :], attn_t[:, b, :], attn_h[:, b % 2, :].bitcast(F32), ALU.subtract)\
                    .then_inc(attn_low, 1)

            def residuals(s):
                t5 = s - 5
                if 0 <= t5 < TILES - 1:
                    pool.wait_ge(z2_ready, t5 + 1)
                    if t5 >= 2:
                        pool.wait_ge(out_stored[t5 % 2], 16 * (t5 // 2))
                    pool.tensor_tensor(out_sb[:, t5 % 2, :], x_sb[:, t5, :], z2[:, t5 % 2, :], ALU.add)\
                        .then_inc(out_ready, 1)
                if s < TILES:
                    pool.wait_ge(z1_ready, s + 1)
                    pool.tensor_tensor(x_sb[:, s, :], x_sb[:, s, :], z1[:, s % 2, :], ALU.add).then_inc(x1_ready, 1)

            for n in range(STEPS):
                u = n - ST_LAG
                if 0 <= u < UNITS:
                    pool.wait_ge(exp_done, 2 * u + 2)
                    blocks = probs[:, u % PRING, 0:3:2, :].rearrange("p a (r q) -> p a r q", r=REP)
                    pool.affine_select(out=blocks, in_=blocks, compare_op=ALU.is_ge, fill=0.0, base=0,
                                       pattern=[[0, 2], [0, REP], [1, P]], channel_multiplier=-1)\
                        .then_inc(probs_masked, 1)
                if n == ROTATE_4:
                    rotate_late()
                if n == SPLIT_HIGH_4:
                    leave_late()
                if n == SPLIT_MIDDLE_4:
                    low_late()
                if n in EARLY:
                    residuals(EARLY[n])
                b, r = divmod(n - PV_LAG - 12, 8)
                if r == 0 and 0 <= b < BATCH - 1:
                    divide(b)
                if r == 2 and 0 <= b < BATCH - 2:
                    attn_low_part(b)
                if n in SPLIT_WEIGHTS:
                    j = SPLIT_WEIGHTS[n]
                    pool.wait_ge(weight_high, j + 1)
                    whole, high, low = quarters[j]
                    pool.tensor_tensor(low, whole, high.bitcast(F32), ALU.subtract).then_inc(weight_low, 1)
            for s in range(2, TILES + 5):
                residuals(s)
                if s == 3:
                    divide(BATCH - 1)
                if s in (2, 4):
                    attn_low_part(BATCH - 3 + s // 2)

        @block.scalar
        def _(act):
            act.wait_ge(pool_const, 1)

            def bring_table(k, t):
                nc.scalar.activation(unused[:, k, t:t + 1], eps_sb[:, 0:1], (ACT.Exp, ACT.Sqrt)[k])

            bring_table(1, TILES)

            def sqrt(k, t):
                act.wait_ge(var_ready[k], t + 1)
                nc.scalar.activation(std[:, k, t:t + 1], mv[:, k, t, 1:2], ACT.Sqrt, bias=eps_sb[:, 0:1])\
                    .then_inc(std_ready[k], 1)

            def copy_xnt(t):
                act.wait_ge(xnt_psum, t + 1)
                nc.scalar.copy(xn_t[:, :, t * P:(t + 1) * P], ps[:, t % 2, :].rearrange("p (c n) -> p c n", c=KC))\
                    .then_inc(xnt_ready, 1)

            def split_high(i):
                a = i % 2
                for ri, ready in enumerate((rot_r, rot_i)):
                    if i == 4:
                        act.wait_ge(late_rotated, ri + 1)
                    else:
                        act.wait_ge(ready, i + 1)
                    if i >= 2:
                        if SETS[i - 2] == "K":
                            act.wait_ge(k_written[0], WRITES_K)
                            act.wait_ge(k_written[1], WRITES_K)
                        else:
                            act.wait_ge(scr_written[i - 2], WRITES_Q)
                    nc.scalar.copy(parts[:, a, ri, 0, :], (late_rot if i == 4 else rot[:, a])[:, ri, :])\
                        .then_inc(part_h, 1)

            def split_middle(i):
                a = i % 2
                for ri in range(2):
                    if i == 4:
                        act.wait_ge(late_left, ri + 1)
                    else:
                        act.wait_ge(resid1[ri], i + 1)
                    nc.scalar.copy(parts[:, a, ri, 1, :], late_resid[ri] if i == 4 else resid[:, a, ri, :])\
                        .then_inc(part_m, 1)

            def copy_v(g):
                act.wait_ge(v_psum, g + 1)
                act.wait_ge(pool_const, 3)
                for i in range(4):
                    last = nc.scalar.copy(v_aug[:, 4 * g + i, :, 0:HEAD_DIM],
                                          ps[:, 6 + g, i * P:(i + 1) * P].rearrange("p (h d) -> p h d", d=HEAD_DIM))
                last.then_inc(v_ready, 1)

            sqrt(0, 0)
            for t in range(1, 4):
                sqrt(0, t)
                copy_xnt(t - 1)
            sqrt(0, 4)
            copy_xnt(3)
            for t in range(5, TILES):
                sqrt(0, t)
            copy_v(0)
            for t in range(4, TILES):
                copy_xnt(t)
            split_high(0)
            split_middle(0)
            copy_v(1)
            for i in range(1, 4):
                split_high(i)
                split_middle(i)

            def normalise(k, t, dst, src, ready):
                nc.scalar.activation(dst, src, ACT.Identity, scale=rstd[:, k, t:t + 1],
                                     bias=nmr[:, k, t:t + 1]).then_inc(ready, 1)

            def attn_high_part(b):
                act.wait_ge(attn_ready, b + 1)
                if b == 0:
                    act.wait_ge(late_rotated, 2)
                if b >= 2:
                    act.wait_ge(wo_psum, 2 * (b - 2) + 2)
                    act.wait_ge(attn_high, b)
                nc.scalar.copy(attn_h[:, b % 2, :], attn_t[:, b, :]).then_inc(attn_high, 1)

            def high_of_transpose(t):
                act.wait_ge(xn1t_psum, t + 1)
                if t >= 2:
                    act.wait_ge(cat_psum, t - 1)
                nc.scalar.copy(xn1_h[:, t % 2, :, :], ps[:, 2, :].rearrange("p (c n) -> p c n", c=KC))\
                    .then_inc(xn1_high, 1)

            def tile_step(s):
                t1, t2, t3, t4, t5 = (s - lag for lag in range(1, 6))
                if 0 <= t2 < TILES and s >= TILES:
                    high_of_transpose(t2)
                if 0 <= t3 < TILES:
                    act.wait_ge(gap_ready, t3 + 1)
                    nc.scalar.activation(gate[:, t3 % 2, 1:2], gate[:, t3 % 2, 0:1], ACT.Exp).then_inc(gexp_ready, 1)
                    bring_table(1, t3)
                if 0 <= t2 < TILES and s < TILES:
                    high_of_transpose(t2)
                if 0 <= t5 < TILES - 1:
                    act.wait_ge(scaled[3], t5 + 1)
                    if t5 >= 2:
                        act.wait_ge(out_ready, t5 - 1)
                    normalise(3, t5, z2[:, t5 % 2, :], y_sb[:, t5 % 2, :], z2_ready)
                if 0 <= t1 < TILES:
                    sqrt(2, t1)
                if s < TILES:
                    sqrt(1, s)
                    act.wait_ge(scaled[1], s + 1)
                    if s >= 2:
                        act.wait_ge(x1_ready, s - 1)
                    normalise(1, s, z1[:, s % 2, :], ps[:, (s + 1) % 2, :], z1_ready)
                if 0 <= t3 < TILES:
                    act.wait_ge(hwt_psum, t3 + 1)
                    if t3 >= 2:
                        act.wait_ge(y_psum, t3 - 1)
                    nc.scalar.copy(hw_t[:, t3 % 2, :], ps[:, 3, 0:P]).then_inc(hwt_ready, 1)
                if 0 <= t4 < TILES:
                    sqrt(3, t4)
                if 0 <= t2 < TILES:
                    bring_table(0, t2)

            for n in range(STEPS):
                u = n - ST_LAG
                if 0 <= u < UNITS:
                    act.wait_ge(t_psum, 2 * u + 1)
                    if u == 0:
                        act.wait_ge(proj_psum, len(SETS))
                        act.wait_ge(v_psum, 2)
                    if u == 2:
                        act.wait_ge(rot_r, 4)
                        act.wait_ge(rot_i, 4)
                    if u == 5:
                        act.wait_ge(part_l[0], 4)
                        act.wait_ge(part_l[1], 4)
                    if u >= PRING:
                        act.wait_ge(o_psum, 2 * ((u - PRING) // 4 + 1))
                    nc.scalar.activation(probs[:, u % PRING, 0, :], ps[:, 3, :], ACT.Exp,
                                         scale=float(HEAD_DIM) ** -0.5).then_inc(exp_done, 1)
                    act.wait_ge(t_psum, 2 * u + 2)
                    nc.scalar.activation(probs[:, u % PRING, 1:3, :], ps[:, 4:6, :], ACT.Exp,
                                         scale=float(HEAD_DIM) ** -0.5).then_inc(exp_done, 1)
                gi, r = divmod(n - MAX_LAG, 4)
                if r == 0 and 0 <= gi < GROUPS:
                    act.wait_ge(mt_psum, gi + 1)
                    if gi >= 2:
                        act.wait_ge(mrow_stacked[gi % 2], 16 * (gi // 2))
                    nc.scalar.copy(mrow[0:PARTS * GROUP_HEADS, gi % 2, :],
                                   ps[0:PARTS * GROUP_HEADS, 0, 0:P].bitcast(BF16)).then_inc(mrow_ready, 1)
                gi, r = divmod(n - PV_LAG, 4)
                if r in (0, 2) and 0 <= gi < VECTOR_OUT:
                    copy_o(act, nc.scalar.copy, gi, r // 2)
                if n in SPLIT_WEIGHTS:
                    j = SPLIT_WEIGHTS[n]
                    if j == 0:
                        act.wait_ge(late_loaded, 80)
                    if j == 4:
                        act.wait_ge(scr_written[3], WRITES_Q)
                        act.wait_ge(scr_written[4], WRITES_Q)
                    whole, high, low = quarters[j]
                    nc.scalar.copy(high, whole).then_inc(weight_high, 1)
                if n == PV_LAG + 13:
                    attn_high_part(0)
                if n == ROTATE_4:
                    act.wait_ge(proj_psum, len(SETS))
                    for i in range(2):
                        nc.scalar.copy(late_set[:, i, :], ps[:, SET_BANKS[4][i], :]).then_inc(late_copied, 1)
                if n == SPLIT_HIGH_4:
                    split_high(4)
                if n == SPLIT_MIDDLE_4:
                    split_middle(4)
                if n in EARLY:
                    tile_step(EARLY[n])
            for s in range(2, TILES + 5):
                tile_step(s)
                if s in (2, 4):
                    attn_high_part(BATCH - 3 + s // 2)

        @block.vector
        def _(dve):
            chained = [0]

            def link(*instructions):
                for ins in instructions:
                    ins.then_inc(dve_chain, 1)
                chained[0] += len(instructions)
                dve.wait_ge(dve_chain, chained[0])

            def ln_stats(k, t, src):
                link(nc.vector.bn_stats(stats[:, k, t, :], src))
                nc.vector.bn_aggr(mv[:, k, t, :], stats[:, k, t, :]).then_inc(var_ready[k], 1)

            def ln_scale(k, t):
                dve.wait_ge(std_ready[k], t + 1)
                link(nc.vector.reciprocal(rstd[:, k, t:t + 1], std[:, k, t:t + 1]))
                nc.vector.scalar_tensor_tensor(out=nmr[:, k, t:t + 1], in0=mv[:, k, t, 0:1], scalar=-1.0,
                                               in1=rstd[:, k, t:t + 1], op0=ALU.mult, op1=ALU.mult)\
                    .then_inc(scaled[k], 1)

            def ln_apply(k, t, dst, src):
                return nc.vector.tensor_scalar(dst, src, mv[:, k, t, 0:1], rstd[:, k, t:t + 1],
                                               ALU.subtract, ALU.mult)

            def input_norm(t):
                ln_scale(0, t)
                ln_apply(0, t, xn_sb[:, t, :], x_sb[:, t, :]).then_inc(xn_ready, 1)

            for t in range(TILES):
                dve.wait_ge(x_loaded[t], 16)
                ln_stats(0, t, x_sb[:, t, :])
                if t >= 1:
                    input_norm(t - 1)
            input_norm(TILES - 1)

            dve.wait_ge(ident_loaded, 16)
            dve.wait_ge(mask_loaded, 16)
            nc.vector.tensor_copy(ident_bf[:, :], ident_sb[:, :]).then_inc(bf_const, 1)
            nc.vector.tensor_copy(mask_bf[:, :, :], mask_f[:, :].unsqueeze(1).broadcast_to([P, REP, P]))\
                .then_inc(bf_const, 1)
            dve.wait_ge(tab_loaded, 16)

            def rope(i, step):
                a = i % 2
                if step == 0:
                    tab = 2 if SETS[i] == "K" else 0
                    cos, sin = (tab_sb[:, tab + j, :].unsqueeze(1).broadcast_to([P, 2, SEQ]) for j in range(2))
                    re, im = (ps[:, bank, :].rearrange("p (b n) -> p b n", b=2) for bank in SET_BANKS[i])
                    dve.wait_ge(proj_psum, i + 1)
                    if i >= 2:
                        dve.wait_ge(rot_r, i - 1)
                        dve.wait_ge(rot_i, i - 1)
                    for j, (val, table) in enumerate(((re, cos), (im, sin), (re, sin), (im, cos))):
                        last = nc.vector.tensor_tensor(rope_t[:, a, j, :].rearrange("p (b n) -> p b n", b=2), val,
                                                       table, ALU.mult)
                    last.then_inc(rope_mul, 1)
                elif step == 1:
                    dve.wait_ge(rope_mul, i + 1)
                    if i >= 2:
                        dve.wait_ge(part_l[0], i - 1)
                    nc.vector.tensor_tensor(rot[:, a, 0, :], rope_t[:, a, 0, :], rope_t[:, a, 1, :], ALU.subtract)\
                        .then_inc(rot_r, 1)
                    dve.wait_ge(part_h, 2 * i + 1)
                    nc.vector.tensor_tensor(resid[:, a, 0, :], rot[:, a, 0, :], parts[:, a, 0, 0, :], ALU.subtract)\
                        .then_inc(resid1[0], 1)
                else:
                    dve.wait_ge(resid1[0], i + 1)
                    dve.wait_ge(part_m, 2 * i + 1)
                    nc.vector.tensor_tensor(parts[:, a, 0, 2, :], resid[:, a, 0, :], parts[:, a, 0, 1, :],
                                            ALU.subtract).then_inc(part_l[0], 1)

            for i in range(3):
                for step in range(3):
                    rope(i, step)
            rope(3, 0)

            def invert(gi):
                rows = slice(64 * (gi % 2), 64 * (gi % 2) + 64)
                dve.wait_ge(den_loaded[gi % 4], 16 * (gi // 4 + 1))
                if gi >= 2:
                    dve.wait_ge(rden_stored[gi % 2], 16 * (gi // 2))
                nc.vector.reciprocal(rden_pk[rows, :], den_pk[rows, :]).then_inc(rden_ready, 1)

            def gating_choice(t):
                ga = gate[:, t % 2, :]
                logits = ps[:, 5 + 2 * (t % 2), YB + EXPERTS * RANK:CATH]
                dve.wait_ge(cat_psum, t + 1)
                link(nc.vector.tensor_copy(ga[:, 48:56], logits))
                link(nc.vector.max(ga[:, 8:16], ga[:, 48:56]))
                nc.vector.tensor_tensor(ga[:, 0:1], ga[:, 9:10], ga[:, 8:9], ALU.subtract).then_inc(gap_ready, 1)
                link(nc.vector.max_index(gate_i[:, t % 2, :], ga[:, 8:16], ga[:, 48:56]))
                link(nc.vector.tensor_copy(ga[:, 16:18], gate_i[:, t % 2, 0:2]))

            def gating_weights(t):
                ga = gate[:, t % 2, :]
                dve.wait_ge(gexp_ready, t + 1)
                link(nc.vector.tensor_scalar(ga[:, 2:3], ga[:, 1:2], 1.0, None, ALU.add))
                link(nc.vector.reciprocal(ga[:, 3:4], ga[:, 2:3]))
                link(nc.vector.tensor_tensor(ga[:, 4:5], ga[:, 1:2], ga[:, 3:4], ALU.mult),
                     nc.vector.tensor_scalar(ga[:, 24:32], iota_sb[:, :], ga[:, 16:17], ga[:, 3:4],
                                             ALU.is_equal, ALU.mult))
                link(nc.vector.tensor_scalar(ga[:, 32:40], iota_sb[:, :], ga[:, 17:18], ga[:, 4:5],
                                             ALU.is_equal, ALU.mult))
                link(nc.vector.tensor_tensor(ga[:, 40:48], ga[:, 24:32], ga[:, 32:40], ALU.add))
                if t >= 2:
                    dve.wait_ge(hwt_psum, t - 1)
                down = ps[:, 5 + 2 * (t % 2), YB:YB + EXPERTS * RANK]
                nc.vector.tensor_tensor(hw[:, t % 2, :].rearrange("p (e r) -> p e r", r=RANK),
                                        down.rearrange("p (e r) -> p e r", r=RANK),
                                        ga[:, 40:48].unsqueeze(2).broadcast_to([P, EXPERTS, RANK]), ALU.mult)\
                    .then_inc(hw_ready, 1)

            def add_bias(t):
                xb = 4 + 2 * (t % 2)
                dve.wait_ge(y_psum, t + 1)
                if t >= 2:
                    dve.wait_ge(z2_ready, t - 1)
                nc.vector.tensor_tensor(y_sb[:, t % 2, 0:CATH], ps[:, xb, 0:CATH], bias_sb[:, 0:CATH], ALU.add)
                nc.vector.tensor_tensor(y_sb[:, t % 2, CATH:DIM], ps[:, xb + 1, 0:YB], bias_sb[:, CATH:DIM],
                                        ALU.add).then_inc(y_ready, 1)

            def tile_step(s):
                t1, t2, t3, t4 = (s - lag for lag in range(1, 5))
                if 0 <= t3 < TILES:
                    gating_choice(t3)
                if t3 == TILES - 1:
                    gating_weights(t3)
                if 0 <= t4 < TILES:
                    add_bias(t4)
                if 0 <= t1 < TILES:
                    dve.wait_ge(x1_ready, t1 + 1)
                    ln_stats(2, t1, x_sb[:, t1, :])
                if 0 <= t3 < TILES - 1:
                    gating_weights(t3)
                if s < TILES:
                    dve.wait_ge(wo_psum, s + 1)
                    ln_stats(1, s, ps[:, (s + 1) % 2, :])
                if 0 <= t2 < TILES:
                    dve.wait_ge(xn1_high, t2 + 1)
                    if t2 >= 2:
                        dve.wait_ge(cat_psum, t2 - 1)
                    nc.vector.tensor_tensor(xn1_l[:, t2 % 2, :, :], ps[:, 2, :].rearrange("p (c n) -> p c n", c=KC),
                                            xn1_h[:, t2 % 2, :, :].bitcast(F32), ALU.subtract).then_inc(xn1_low, 1)
                if s < TILES:
                    ln_scale(1, s)
                if 0 <= t1 < TILES:
                    ln_scale(2, t1)
                    if t1 >= 2:
                        dve.wait_ge(xn1t_psum, t1 - 1)
                    ln_apply(2, t1, xn1_sb[:, t1 % 2, :], x_sb[:, t1, :]).then_inc(xn1_ready, 1)
                if 0 <= t4 < TILES:
                    dve.wait_ge(y_ready, t4 + 1)
                    ln_stats(3, t4, y_sb[:, t4 % 2, :])
                    if t4 < TILES - 1:
                        ln_scale(3, t4)
                    else:
                        dve.wait_ge(std_ready[3], TILES)
                        link(nc.vector.reciprocal(rstd[:, 3, t4:t4 + 1], std[:, 3, t4:t4 + 1]))
                        dve.wait_ge(out_ready, t4 - 1)
                        link(ln_apply(3, t4, z2[:, t4 % 2, :], y_sb[:, t4 % 2, :]))
                        dve.wait_ge(out_stored[t4 % 2], 16 * (t4 // 2))
                        nc.vector.tensor_tensor(out_sb[:, t4 % 2, :], x_sb[:, t4, :], z2[:, t4 % 2, :], ALU.add)\
                            .then_inc(last_ready, 1)

            for n in range(STEPS):
                gi, k = divmod(n, GROUP_KV)
                if n < UNITS:
                    heads = slice(k * REP, (k + 1) * REP)
                    dve.wait_ge(s0_psum, n + 1)
                    nc.vector.tensor_reduce(nmax[:, gi % 2, 0, heads], ps[:, 0, :].rearrange("p (r k) -> p r k", r=REP),
                                            AX.X, ALU.max, negate=True).then_inc(s0_free, 1)
                    dve.wait_ge(s12_psum, n + 1)
                    nc.vector.tensor_reduce(nmax[:, gi % 2, 1, heads],
                                            ps[:, 1:3, :].rearrange("p a (r k) -> p r a k", r=REP),
                                            AX.XY, ALU.max, negate=True).then_inc(s12_free, 1)
                if k == 0 and 1 <= gi <= GROUPS:
                    full, left = nmax[:, (gi - 1) % 2, :, :], nmax_r[:, (gi - 1) % 2, :, :]
                    high, mid, low = (nmax_p[:, :, j, :] for j in range(PARTS))
                    dve.wait_ge(s12_free, n)
                    if gi >= 2:
                        dve.wait_ge(mt_psum, gi - 1)
                    link(nc.vector.tensor_copy(high, full))
                    link(nc.vector.tensor_tensor(left, full, high, ALU.subtract))
                    link(nc.vector.tensor_copy(mid, left))
                    nc.vector.tensor_tensor(low, left, mid, ALU.subtract).then_inc(nmax_split, 1)
                if n in ROPE_3:
                    rope(3, ROPE_3[n])
                if n == PV_LAG + 21:
                    dve.wait_ge(attn_ready, 2)
                    dve.wait_ge(attn_high, 1)
                    nc.vector.tensor_copy(attn_h[:, 1, :], attn_t[:, 1, :]).then_inc(attn_high, 1)
                gi, r = divmod(n - PV_LAG, 4)
                if r in (0, 2) and VECTOR_OUT <= gi < GROUPS:
                    copy_o(dve, nc.vector.tensor_copy, gi, r // 2)
                gi, r = divmod(n - PV_LAG - 6, 4)
                if r == 0 and 0 <= gi < GROUPS - 1:
                    invert(gi)
                if n in EARLY:
                    tile_step(EARLY[n])
            dve.wait_ge(late_loaded, 80)
            for s in range(2, TILES + 4):
                tile_step(s)
                if s == 2:
                    invert(GROUPS - 1)

        @block.tensor
        def _(pe):
            pe.wait_ge(ident_loaded, 16)

            def turn_x(t):
                pe.wait_ge(xn_ready, t + 1)
                if t >= 2:
                    pe.wait_ge(xnt_ready, t - 1)
                for c in range(KC):
                    last = nc.tensor.transpose(ps[:, t % 2, c * P:(c + 1) * P], xn_sb[:, t, c * P:(c + 1) * P],
                                               ident_sb[:, :])
                last.then_inc(xnt_psum, 1)

            def project(i, first=0, count=2 * KC):
                if i >= 3:
                    pe.wait_ge(rope_mul, i - 2)
                if SETS[i] == "K":
                    pe.wait_ge(wk_loaded, 16)
                    pe.wait_ge(xnt_ready, TILES)
                    for ri in range(2):
                        for c in range(KC):
                            for half in range(2):
                                last = nc.tensor.matmul(ps[64 * half:64 * half + 64, SET_BANKS[i][ri], :],
                                                        wk_sb[:, c, 64 * ri:64 * ri + 64],
                                                        xn_t[:, c, half * HALF:(half + 1) * HALF],
                                                        start=(c == 0), stop=(c == KC - 1))
                else:
                    half, g = SETS[i]
                    pe.wait_ge(wq_loaded[g], 16)
                    if i == 2:
                        pe.wait_ge(v_ready, 2)
                    pe.wait_ge(xnt_ready, 4 * half + 4)
                    for m in range(first, first + count):
                        ri, c = divmod(m, KC)
                        col = (2 * g + ri) * P
                        last = nc.tensor.matmul(ps[:, SET_BANKS[i][ri], :], wq_sb[:, c, col:col + P],
                                                xn_t[:, c, half * HALF:(half + 1) * HALF],
                                                start=(c == 0), stop=(c == KC - 1))
                if first + count == 2 * KC:
                    last.then_inc(proj_psum, 1)

            def project_v(t):
                pe.wait_ge(wv_loaded, 16)
                pe.wait_ge(xnt_ready, t + 1)
                for c in range(KC):
                    last = nc.tensor.matmul(ps[:, 6 + t // 4, (t % 4) * P:(t % 4 + 1) * P],
                                            xn_t[:, c, t * P:(t + 1) * P], wv_sb[:, c, :],
                                            start=(c == 0), stop=(c == KC - 1))
                if t % 4 == 3:
                    last.then_inc(v_psum, 1)

            def turn_and_project_v(first):
                for t in range(first, first + 4):
                    turn_x(t)
                    if t > first:
                        project_v(t - 1)
                project_v(first + 3)

            turn_and_project_v(0)
            project(0)
            turn_and_project_v(4)
            for i in range(1, 4):
                project(i)
            project(4, 0, 2 * KC - sum(MATMULS_4))

            def scores(n):
                gi, k = divmod(n, GROUP_KV)
                slot = gi % RING
                if k == 0:
                    pe.wait_ge(qk_loaded[slot], 32 * (gi // RING + 1))
                if n == 0:
                    pe.wait_ge(bf_const, 2)
                    pe.wait_ge(v_ready, 2)
                    pe.wait_ge(rope_mul, 4)
                    pe.wait_ge(pool_const, 4)
                else:
                    pe.wait_ge(s0_free, n)
                gj, r = divmod(n - MAX_LAG - 1, 4)
                if r == 0 and 0 <= gj < GROUPS:
                    pe.wait_ge(mrow_ready, gj + 1)
                nc.tensor.matmul(ps[:, 0, :], ident_bf[:, :], mask_bf[:, :, :].rearrange("p r k -> p (r k)"),
                                 start=True, stop=False, skip_group_check=True)
                for r in range(REP):
                    h = k * REP + r
                    last = nc.tensor.matmul(ps[:, 0, r * P:(r + 1) * P], qst[0:SROWS, slot, h, 0:P],
                                            kst[0:SROWS, slot, k, 0:P], start=False, stop=(r == REP - 1),
                                            skip_group_check=True)
                last.then_inc(s0_psum, 1)

            def scores_more(n):
                gi, k = divmod(n, GROUP_KV)
                slot = gi % RING
                if n >= 1:
                    pe.wait_ge(s12_free, n)
                nc.tensor.matmul(ps[:, 2, :], ident_bf[:, :], mask_bf[:, :, :].rearrange("p r k -> p (r k)"),
                                 start=True, stop=False, skip_group_check=True)
                for r in range(REP):
                    h = k * REP + r
                    for kt in range(2):
                        last = nc.tensor.matmul(ps[:, 1 + kt, r * P:(r + 1) * P], qst[0:SROWS, slot, h, P:2 * P],
                                                kst[0:SROWS, slot, k, kt * P:(kt + 1) * P], start=(kt == 0),
                                                stop=(r == REP - 1), skip_group_check=True)
                last.then_inc(s12_psum, 1)

            def turn_max(gi, n):
                pe.wait_ge(nmax_split, gi + 1)
                pe.wait_ge(s0_free, min(n + 1, UNITS))
                for qt in range(2):
                    last = nc.tensor.transpose(ps[0:PARTS * GROUP_HEADS, 0, qt * 64:(qt + 1) * 64].bitcast(BF16),
                                               nmax_p[:, qt, :, :].rearrange("p a h -> p (a h)"), ident_bf[:, :])
                last.then_inc(mt_psum, 1)

            def scores_t(u):
                gi, k = divmod(u, GROUP_KV)
                slot = gi % RING
                if k == 0:
                    pe.wait_ge(mrow_stacked[gi % 2], 16 * (gi // 2 + 1))
                if u == 0:
                    pe.wait_ge(late_copied, 2)
                for j, (kt, qt) in enumerate(((0, 0), (0, 1), (1, 1))):
                    if u >= 1 and j < 2:
                        pe.wait_ge(exp_done, 2 * u - 1 + j)
                    last = nc.tensor.matmul(ps[:, 3 + j, :], kst[0:TROWS, slot, k, kt * P:(kt + 1) * P],
                                            qst[0:TROWS, slot, k * REP:(k + 1) * REP, qt * P:(qt + 1) * P],
                                            start=True, stop=True)
                    if j != 1:
                        last.then_inc(t_psum, 1)

            def attend(gi, piece):
                b, g = divmod(gi, 2)
                qt, kt = ((0, 0), (1, 0), (1, 1))[piece]
                pe.wait_ge(probs_masked, 4 * gi + 4)
                if gi >= 1 and kt == 0:
                    wait_o(pe, 2 * gi - 1 + qt)
                for j in range(GROUP_KV):
                    u = gi * GROUP_KV + j
                    last = nc.tensor.matmul(ps[32 * j:32 * j + 32, 6 + qt, :],
                                            v_aug[:, 2 * b + kt, g * GROUP_KV + j, :],
                                            probs[:, u % PRING, qt + kt, :],
                                            start=(kt == 0), stop=(kt == qt))
                if kt == qt:
                    last.then_inc(o_psum, 1)

            def project_out(t):
                if t == 0:
                    pe.wait_ge(weight_low, 8)
                    pe.wait_ge(s12_free, UNITS)
                if t == 1:
                    pe.wait_ge(mrow_ready, GROUPS)
                pe.wait_ge(attn_low, t // 2 + 1)
                if t >= 2:
                    pe.wait_ge(z1_ready, t - 1)
                b = t // 2
                terms = [(attn, w, r) for attn, w in ((attn_h[:, b % 2, :], wo_h), (attn_h[:, b % 2, :], wo_l),
                                                      (attn_l[:, b, :], wo_h)) for r in range(REP)]
                for i, (attn, w, r) in enumerate(terms):
                    col = r * SEQ + (t % 2) * P
                    last = nc.tensor.matmul(ps[:, (t + 1) % 2, :], attn[:, col:col + P], w[:, r, :],
                                            start=(i == 0), stop=(i == len(terms) - 1))
                last.then_inc(wo_psum, 1)

            def turn_mid(t):
                pe.wait_ge(xn1_ready, t + 1)
                if t >= 1:
                    pe.wait_ge(xn1_low, t)
                for c in range(KC):
                    last = nc.tensor.transpose(ps[:, 2, c * P:(c + 1) * P], xn1_sb[:, t % 2, c * P:(c + 1) * P],
                                               ident_sb[:, :])
                last.then_inc(xn1t_psum, 1)

            def base_down_router(t, term):
                if term == 0:
                    pe.wait_ge(xn1_high, t + 1)
                    if t >= 2:
                        pe.wait_ge(y_ready, t - 1)
                if term == 2:
                    pe.wait_ge(xn1_low, t + 1)
                act_part, w = ((xn1_h, wcat_h), (xn1_h, wcat_l), (xn1_l, wcat_h))[term]
                for hf in range(2):
                    for c in range(KC):
                        last = nc.tensor.matmul(ps[:, 4 + 2 * (t % 2) + hf, 0:CATH], act_part[:, t % 2, c, :],
                                                w[:, c, hf * CATH:(hf + 1) * CATH], start=(term == 0 and c == 0),
                                                stop=(term == 2 and hf == 1 and c == KC - 1), skip_group_check=True)
                if term == 2:
                    last.then_inc(cat_psum, 1)

            def turn_hw(t):
                pe.wait_ge(hw_ready, t + 1)
                if t >= 1:
                    pe.wait_ge(hwt_ready, t)
                nc.tensor.transpose(ps[:, 3, 0:P], hw[:, t % 2, :], ident_sb[:, :]).then_inc(hwt_psum, 1)

            def up_projection(t):
                pe.wait_ge(hwt_ready, t + 1)
                nc.tensor.matmul(ps[:, 4 + 2 * (t % 2), 0:CATH], hw_t[:, t % 2, :], lora_b_sb[:, 0:CATH],
                                 start=False, stop=True, skip_group_check=True)
                nc.tensor.matmul(ps[:, 5 + 2 * (t % 2), 0:YB], hw_t[:, t % 2, :], lora_b_sb[:, CATH:DIM],
                                 start=False, stop=True, skip_group_check=True).then_inc(y_psum, 1)

            def tile_step(s):
                t2, t3 = s - 2, s - 3
                if s == 2:
                    project_out(s)
                    pe.wait_ge(exp_done, 2 * UNITS)
                    wait_o(pe, 2 * GROUPS)
                if 0 <= t2 < TILES:
                    turn_mid(t2)
                if 3 <= s < TILES:
                    project_out(s)
                if 0 <= t2 < TILES:
                    base_down_router(t2, 0)
                if 0 <= t3 < TILES:
                    turn_hw(t3)
                if 0 <= t2 < TILES:
                    base_down_router(t2, 1)
                    base_down_router(t2, 2)
                if 0 <= t3 < TILES:
                    up_projection(t3)

            for n in range(STEPS):
                if n < UNITS:
                    scores(n)
                if 0 <= n - ST_LAG < UNITS:
                    scores_t(n - ST_LAG)
                if n < UNITS:
                    scores_more(n)
                if n < len(MATMULS_4):
                    project(4, 2 * KC - sum(MATMULS_4[n:]), MATMULS_4[n])
                gi, r = divmod(n - MAX_LAG, 4)
                if r == 0 and 0 <= gi < GROUPS:
                    turn_max(gi, n)
                gi, r = divmod(n - PV_LAG, 4)
                if r < 3 and 0 <= gi < GROUPS:
                    attend(gi, r)
                if n in EARLY_OUT:
                    project_out(EARLY_OUT[n])
            for s in range(2, TILES + 3):
                tile_step(s)


def rotary_tables():
    freqs = 1.0 / np.float32(10000.0) ** (np.arange(0, HEAD_DIM, 2, dtype=np.float32) / HEAD_DIM)
    angles = (np.arange(SEQ, dtype=np.float32)[:, None] * freqs.astype(np.float32)[None]).astype(np.float32)
    rows_q = np.arange(P) // GROUP_HEADS
    rows_k = (np.arange(P) % 64) // KV_HEADS
    return np.stack([f(angles).T[rows] for rows in (rows_q, rows_k) for f in (np.cos, np.sin)], axis=1)\
        .astype(np.float32)


def kernel(L0_attn_x, L0_attn_wq, L0_attn_wk, L0_attn_wv, L0_attn_wo, L0_ffn_W_base, L0_ffn_b_base, L0_ffn_W_gate,
           L0_ffn_A, L0_ffn_B):
    from concourse import bacc
    from concourse.bass_utils import run_bass_kernel_spmd

    def arr(a):
        return np.asarray(a)

    wq = arr(L0_attn_wq).reshape(DIM, 2, GROUP_HEADS, FREQS, 2).transpose(0, 1, 4, 3, 2).reshape(DIM, DIM)
    wk = arr(L0_attn_wk).reshape(DIM, KV_HEADS, FREQS, 2).transpose(0, 3, 2, 1).reshape(DIM, P)
    wo = arr(L0_attn_wo).reshape(KV_HEADS, REP, HEAD_DIM, DIM).transpose(1, 0, 2, 3).reshape(DIM, DIM)
    wcat = np.concatenate([arr(L0_ffn_W_base).T, arr(L0_ffn_A).reshape(EXPERTS * RANK, DIM).T,
                           arr(L0_ffn_W_gate).T], axis=1)
    lora_b = arr(L0_ffn_B).transpose(0, 2, 1).reshape(EXPERTS * RANK, DIM)
    later = np.arange(P)[None, :] > np.arange(P)[:, None]
    arrays = {
        "x": arr(L0_attn_x).reshape(TOKENS, DIM), "wq": wq, "wk": wk, "wv": arr(L0_attn_wv), "wo": wo,
        "wcat": wcat, "lora_b": lora_b, "bias": arr(L0_ffn_b_base), "tables": rotary_tables(),
        "ident": np.eye(P, dtype=np.float32), "maskq": np.where(later, np.float32(MASKED), np.float32(0)),
        "iota": np.tile(np.arange(EXPERTS, dtype=np.float32), (P, 1)),
    }
    arrays = {n: np.ascontiguousarray(a) for n, a in arrays.items()}
    nc = bacc.Bacc("TRN2", target_bir_lowering=False, num_devices=1)
    args = [nc.dram_tensor(n, a.shape, mybir.dt.from_np(a.dtype), kind="ExternalInput").ap() for n, a in arrays.items()]
    out = nc.dram_tensor("out", [TOKENS, DIM], F32, kind="ExternalOutput").ap()
    build(nc, *args, out)
    r = run_bass_kernel_spmd(nc, [arrays], core_ids=[0])
    return r.results[0]["out"].reshape(BATCH, SEQ, DIM)
```
